# Optimizing a Trainium2 kernel written in Bass

```python
import numpy as np
import jax
import jax.numpy as jnp

def _softmax(x, axis=-1):
    return jax.nn.softmax(x, axis=axis)

def _gelu(x):
    return jax.nn.gelu(x, approximate=True)

def _silu(x):
    return jax.nn.silu(x)

def _sigmoid(x):
    return jax.nn.sigmoid(x)

def _layernorm(x, axis=-1, eps=1e-05):
    m = jnp.mean(x, axis=axis, keepdims=True)
    v = jnp.var(x, axis=axis, keepdims=True)
    return (x - m) / jnp.sqrt(v + eps)

def _scatter_add(tgt, idx, src, axis=0):
    return tgt.at[idx].add(src)

def _segment_sum(src, seg, n):
    return jax.ops.segment_sum(src, seg, n)
kernel_name = 'mk_sandwich_d1_jaxref_r2_81952d'

def setup_inputs(seed: int=0):
    np.random.seed(seed)
    _w = jnp.asarray

    def _L0_attn_setup():
        import jax, jax.numpy as jnp
        import numpy as np
        D_MODEL = 512
        D_HIDDEN = 128
        key = jax.random.key(seed)
        ks = jax.random.split(key, 10)
        B, T = (4, 2048)
        s = lambda fan_in: 1.0 / np.sqrt(fan_in)
        return {'x': jax.random.normal(ks[0], (B, T, D_MODEL), dtype=jnp.float32), 'A': jnp.log(jnp.arange(1, D_HIDDEN + 1, dtype=jnp.float32)), 'Wb': jax.random.uniform(ks[1], (D_MODEL, D_HIDDEN), jnp.float32, -s(D_MODEL), s(D_MODEL)), 'bb': jax.random.uniform(ks[2], (D_HIDDEN,), jnp.float32, -s(D_MODEL), s(D_MODEL)), 'Wc': jax.random.uniform(ks[3], (D_HIDDEN, D_MODEL), jnp.float32, -s(D_HIDDEN), s(D_HIDDEN)), 'bc': jax.random.uniform(ks[4], (D_MODEL,), jnp.float32, -s(D_HIDDEN), s(D_HIDDEN)), 'Wd': jax.random.uniform(ks[5], (D_MODEL, D_MODEL), jnp.float32, -s(D_MODEL), s(D_MODEL)), 'bd': jax.random.uniform(ks[6], (D_MODEL,), jnp.float32, -s(D_MODEL), s(D_MODEL)), 'Wdelta': jax.random.uniform(ks[7], (D_MODEL, D_HIDDEN), jnp.float32, -s(D_MODEL), s(D_MODEL)), 'bdelta': jax.random.uniform(ks[8], (D_HIDDEN,), jnp.float32, -s(D_MODEL), s(D_MODEL))}
    _L0_attn_in = _L0_attn_setup()

    def _L0_ffn_setup():
        import jax, jax.numpy as jnp
        import numpy as np
        DIM = 512

        def _reference_tuple_inner(x, W_r, W_k, W_v, mu_r, mu_k):
            B, T, C = x.shape
            x_prev = jnp.concatenate([jnp.zeros((B, 1, C), x.dtype), x[:, :-1, :]], axis=1)
            xr = mu_r * x + (1.0 - mu_r) * x_prev
            xk = mu_k * x + (1.0 - mu_k) * x_prev
            r = jax.nn.sigmoid(jnp.einsum('btc,dc->btd', xr, W_r))
            k = jnp.einsum('btc,dc->btd', xk, W_k)
            k_act = jnp.square(jax.nn.relu(k))
            out = r * jnp.einsum('btc,dc->btd', k_act, W_v)
            new_state = x[:, -1, :]
            return (out, new_state)
        key = jax.random.key(seed)
        ks = jax.random.split(key, 6)
        B, T, C = (8, 1024, DIM)
        x = jax.random.normal(ks[0], (B, T, C), dtype=jnp.float32)
        s = 1.0 / np.sqrt(C)
        W_r = jax.random.uniform(ks[1], (C, C), jnp.float32, -s, s)
        W_k = jax.random.uniform(ks[2], (C, C), jnp.float32, -s, s)
        W_v = jax.random.uniform(ks[3], (C, C), jnp.float32, -s, s)
        mu_r = jax.random.uniform(ks[4], (C,), jnp.float32)
        mu_k = jax.random.uniform(ks[5], (C,), jnp.float32)
        return {'x': x, 'W_r': W_r, 'W_k': W_k, 'W_v': W_v, 'mu_r': mu_r, 'mu_k': mu_k}
    _L0_ffn_in = _L0_ffn_setup()
    _d = {'L0_attn_x': _L0_attn_in['x'], 'L0_attn_A': _L0_attn_in['A'], 'L0_attn_Wb': _L0_attn_in['Wb'], 'L0_attn_bb': _L0_attn_in['bb'], 'L0_attn_Wc': _L0_attn_in['Wc'], 'L0_attn_bc': _L0_attn_in['bc'], 'L0_attn_Wd': _L0_attn_in['Wd'], 'L0_attn_bd': _L0_attn_in['bd'], 'L0_attn_Wdelta': _L0_attn_in['Wdelta'], 'L0_attn_bdelta': _L0_attn_in['bdelta'], 'L0_ffn_W_r': _L0_ffn_in['W_r'], 'L0_ffn_W_k': _L0_ffn_in['W_k'], 'L0_ffn_W_v': _L0_ffn_in['W_v'], 'L0_ffn_mu_r': _L0_ffn_in['mu_r'], 'L0_ffn_mu_k': _L0_ffn_in['mu_k']}
    _x0 = _d['L0_attn_x']
    _d['L0_attn_x'] = jax.random.normal(jax.random.fold_in(jax.random.key(seed), 1), (2, 4096, 512), dtype=_x0.dtype)
    del _x0
    return _d

def reference(L0_attn_x, L0_attn_A, L0_attn_Wb, L0_attn_bb, L0_attn_Wc, L0_attn_bc, L0_attn_Wd, L0_attn_bd, L0_attn_Wdelta, L0_attn_bdelta, L0_ffn_W_r, L0_ffn_W_k, L0_ffn_W_v, L0_ffn_mu_r, L0_ffn_mu_k):

    def _L0_attn_ref(x, A, Wb, bb, Wc, bc, Wd, bd, Wdelta, bdelta):
        import jax, jax.numpy as jnp
        import numpy as np
        D_MODEL = 512
        D_HIDDEN = 128
        delta = jax.nn.softplus(jnp.einsum('btc,ch->bth', x, Wdelta) + bdelta)
        A_log = -jax.nn.softplus(A)
        A_bar_log = delta * A_log
        B_bar = delta * (jnp.einsum('btc,ch->bth', x, Wb) + bb)
        A_log_cum = jnp.clip(jnp.cumsum(A_bar_log, axis=1), -20.0, 20.0)
        A_log_cum_shifted = jnp.concatenate([jnp.zeros_like(A_log_cum[:, :1, :]), A_log_cum[:, :-1, :]], axis=1)
        B_shift = B_bar * jnp.exp(-A_log_cum_shifted)
        h = jnp.exp(A_log_cum) * jnp.cumsum(B_shift, axis=1)
        out = jnp.einsum('bth,hc->btc', h, Wc) + bc + jnp.einsum('btc,cd->btd', x, Wd) + bd
        return out

    def _L0_ffn_ref(x, W_r, W_k, W_v, mu_r, mu_k):
        import jax, jax.numpy as jnp
        import numpy as np
        DIM = 512

        def _reference_tuple_inner(x, W_r, W_k, W_v, mu_r, mu_k):
            B, T, C = x.shape
            x_prev = jnp.concatenate([jnp.zeros((B, 1, C), x.dtype), x[:, :-1, :]], axis=1)
            xr = mu_r * x + (1.0 - mu_r) * x_prev
            xk = mu_k * x + (1.0 - mu_k) * x_prev
            r = jax.nn.sigmoid(jnp.einsum('btc,dc->btd', xr, W_r))
            k = jnp.einsum('btc,dc->btd', xk, W_k)
            k_act = jnp.square(jax.nn.relu(k))
            out = r * jnp.einsum('btc,dc->btd', k_act, W_v)
            new_state = x[:, -1, :]
            return (out, new_state)
        return _reference_tuple_inner(x, W_r, W_k, W_v, mu_r, mu_k)[0]
    x = L0_attn_x
    x = x + _layernorm(_L0_attn_ref(_layernorm(x, axis=-1), L0_attn_A, L0_attn_Wb, L0_attn_bb, L0_attn_Wc, L0_attn_bc, L0_attn_Wd, L0_attn_bd, L0_attn_Wdelta, L0_attn_bdelta), axis=-1)
    x = x + _layernorm(_L0_ffn_ref(_layernorm(x, axis=-1), L0_ffn_W_r, L0_ffn_W_k, L0_ffn_W_v, L0_ffn_mu_r, L0_ffn_mu_k), axis=-1)
    return x

_drawn_inputs = setup_inputs


def setup_inputs(seed=0):
    import zlib

    import numpy as np

    out = dict(_drawn_inputs(seed))
    spreads = {}
    factors = {'L0_attn_bc': 8.0, 'L0_attn_bd': 8.0, 'L0_attn_bdelta': 3.786}
    for name, (base, spread) in spreads.items():
        noise = np.random.default_rng([zlib.crc32(name.encode()), seed]).standard_normal(out[name].shape)
        drawn = base * np.exp(spread * noise) if base else spread * noise
        out[name] = jnp.asarray(drawn.astype(out[name].dtype))
    for name, factor in factors.items():
        out[name] = (out[name] * factor).astype(out[name].dtype)
    return out
```

```python
from contextlib import ExitStack

import concourse.bass as bass
from concourse import mybir

ALU = mybir.AluOpType
ACT = mybir.ActivationFunctionType
F32 = mybir.dt.float32
F32R = mybir.dt.float32r

P = 128
TILE = 512
TB = TILE // P
EPS = 1e-5
CLIP = 20.0
SOFTPLUS_MAX = 30.0


def state_space_mixer_and_channel_mixer(nc, x_in, vectors, bc, bd, w_delta, w_b, w_c, w_d, w_r, w_k, w_v, out):
    NB, T, DM = x_in.shape
    DH = w_c.shape[0]
    CH = DM // P
    NT = NB * T // TILE
    assert NB == 2 and DH == P and DM == 512 and NT % 2 == 0

    x_d = x_in.rearrange("b (n p) d -> p (b n) d", p=P)
    out_d = out.rearrange("b (n p) d -> p (b n) d", p=P)

    with ExitStack() as ctx:
        def sb(name, shape, dt=F32):
            return ctx.enter_context(nc.sbuf_tensor(name, shape, dt))

        def bank(name):
            return ctx.enter_context(nc.psum_tensor(name, [P, 512], F32))

        def sem(name):
            return ctx.enter_context(nc.semaphore(name))

        wdelta_hi, wdelta_lo = sb("wdelta_hi", [P, CH, DH], F32R), sb("wdelta_lo", [P, CH, DH], F32R)
        wb_hi, wb_lo = sb("wb_hi", [P, CH, DH], F32R), sb("wb_lo", [P, CH, DH], F32R)
        wc_hi, wc_lo = sb("wc_hi", [P, DM], F32R), sb("wc_lo", [P, DM], F32R)
        wd_hi, wd_lo = sb("wd_hi", [P, CH, DM], F32R), sb("wd_lo", [P, CH, DM], F32R)
        wr_hi, wr_lo = sb("wr_hi", [P, CH, DM], F32R), sb("wr_lo", [P, CH, DM], F32R)
        wk_hi, wk_lo = sb("wk_hi", [P, CH, DM], F32R), sb("wk_lo", [P, CH, DM], F32R)
        wv_hi, wv_lo = sb("wv_hi", [P, CH, DM], F32R), sb("wv_lo", [P, CH, DM], F32R)
        bias_rows = sb("bias_rows", [P, DM], F32R)
        ones = sb("ones", [P, P], F32R)
        ident = sb("ident", [P, P])
        vecs = sb("vecs", [P, vectors.shape[1]])
        x = sb("x", [P, 2, TB, DM])
        x1 = sb("x1", [P, 2, TB, DM])
        xn = sb("xn", [P, 2, DM])
        xT_hi, xT_lo = sb("xT_hi", [P, CH, TILE], F32R), sb("xT_lo", [P, CH, TILE], F32R)
        x1n = sb("x1n", [P, TB, DM])
        x1T = sb("x1T", [P, CH, TILE + 1])
        mix_hi, mix_lo = sb("mix_hi", [P, CH, TILE], F32R), sb("mix_lo", [P, CH, TILE], F32R)
        ka_hi, ka_lo = sb("ka_hi", [P, CH, TILE], F32R), sb("ka_lo", [P, CH, TILE], F32R)
        sig = sb("sig", [P, TB, DM])
        work = sb("work", [P, 4, TILE])
        relu = work[:, 0:2, :]
        mixf = work[:, 2:4, :]
        soft = sb("soft", [P, TILE])
        delta = sb("delta", [P, TILE])
        bbar = sb("bbar", [P, TILE])
        cum = sb("cum", [P, TILE + 1])
        h_hi, h_lo = sb("h_hi", [P, TILE], F32R), sb("h_lo", [P, TILE], F32R)
        smalls = sb("smalls", [P, 4 * 2 * 6 + 4 * TB * 5 + 3 * TB + 2 + 2 * NB + NB * CH])
        taken = [0]

        def small(*shape):
            n = 1
            for k in shape:
                n *= k
            part = smalls[:, taken[0]:taken[0] + n]
            taken[0] += n
            names = " ".join("abc"[:len(shape)])
            return part.rearrange(f"p ({names}) -> p {names}", **dict(zip("abc", shape))) if len(shape) > 1 else part

        stats = small(4, 2, 6)
        mv = small(4, TB, 2)
        vare, rstd, nmr = small(4, TB), small(4, TB), small(4, TB)
        mhalf, epsilon, minus1 = small(TB), small(TB), small(TB)
        a_neg, a_tmp = small(1), small(1)
        cum_carry, h_carry = small(NB), small(NB)
        x1T_carry = small(NB, CH)

        A_v, bb_v, bdelta_v = vecs[:, 0:1], vecs[:, 1:2], vecs[:, 2:3]
        mu_r, mu_k = vecs[:, 3:3 + CH], vecs[:, 3 + CH:3 + 2 * CH]

        kr_bank = [bank("kr0"), bank("kr1")]
        av_bank = [bank("av0"), bank("av1")]
        tr_bank = [bank("tr0"), bank("tr1")]
        z_bank, b_bank = bank("zb"), bank("bb")

        s_vec, s_w = sem("vectors_loaded"), [sem(f"weight{i}_loaded") for i in range(9)]
        s_stored = [sem("stored_even"), sem("stored_odd")]
        s_ident, s_const, s_asoft = sem("ident_ready"), sem("constants_ready"), sem("a_softplus")
        s_wsplit, s_whi, s_bias = sem("weights_split"), sem("weight_hi"), sem("bias_rows")
        nmp = [sem(f"ln{i + 1}_mean_rstd") for i in range(4)]
        s_xl = [sem("x_loaded_even"), sem("x_loaded_odd")]
        z_ready, b_ready = sem("z_ready"), sem("b_ready")
        k_ready, att_ready, t1_ready = sem("k_ready"), sem("att_ready"), sem("t1_ready")
        r_ready, t2_ready, v_ready = sem("r_ready"), sem("t2_ready"), sem("v_ready")
        zc_done, e_done, l_done = sem("z_clamped"), sem("exp_done"), sem("log_done")
        delta_done, a_done, cum_done, cumc_done = sem("delta_done"), sem("a_done"), sem("cum_done"), sem("cum_carried")
        c_done, dc_done, g_done, bbar_done = sem("clip_done"), sem("step_done"), sem("decay_done"), sem("bbar_done")
        col0_done, h_done, hhi_done, h_split = sem("cum_col0"), sem("h_done"), sem("h_hi_done"), sem("h_split")
        relu_done, kahi_done, sq_done, ka_split = sem("relu_done"), sem("ka_hi_done"), sem("square_done"), sem("ka_split")
        bn1, mv1, bn2, mv2 = sem("bn1"), sem("mv1"), sem("bn2"), sem("mv2")
        bn3, mv3, bn4, mv4 = sem("bn3"), sem("mv3"), sem("bn4"), sem("mv4")
        rs = [sem(f"ln{i + 1}_rstd") for i in range(4)]
        ve = [sem(f"ln{i + 1}_vare") for i in range(4)]
        nm = [sem(f"ln{i + 1}_scales") for i in range(4)]
        xn_done, xhi_done, xlo_done = sem("xn_done"), sem("xT_hi_done"), sem("xT_lo_done")
        u2_done, x1_done, x1n_done, evac_done = sem("u2_done"), sem("x1_done"), sem("x1n_done"), sem("x1T_done")
        x1c_done = sem("x1T_col0")
        diff_done, mixf_done, mixhi_done, mix_split = sem("diff_done"), sem("mixf_done"), sem("mix_hi_done"), sem("mix_split")
        sig_done, w_done, u4_done, y_done = sem("sig_done"), sem("w_done"), sem("u4_done"), sem("y_done")

        block = ctx.enter_context(nc.Block())

        def run(eng, first, step, last):
            first()
            step(1, 1, 0, True)
            with eng.Fori(1, NT // 2 - 1) as i:
                step(2 * i, 0, i, True)
                step(2 * i + 1, 1, i, True)
            step(NT - 2, 0, NT // 2 - 1, True)
            step(NT - 1, 1, NT // 2 - 1, False)
            last()

        WEIGHTS = [(w_delta, x1n[:, 0, :]), (w_b, x1n[:, 1, :]), (w_d, x1[:, 0, :, :]), (w_c, x1n[:, 2, :]),
                   (bc, x1n[:, 3, :]), (bd, soft[:, :]), (w_k, x1[:, 1, :, :]), (w_r, sig[:, :, :]), (w_v, work[:, :, :])]
        STAGED = [s for _, s in WEIGHTS]
        SPLITS = [0, 1, 2, 3, 6, 7, 8]
        CONSTANTS = 9

        @block.sync
        def _(sp):
            def load_x(par, block):
                sp.dma_start(x[:, par, :, :], x_d[:, bass.ds(block + par * T // P, TB), :]).then_inc(s_xl[par], 16)

            def load_weight(n):
                src, dst = WEIGHTS[n]
                sp.dma_start(dst, src).then_inc(s_w[n], 16)

            load_x(0, 0)
            sp.dma_start(vecs[:, :], vectors).then_inc(s_vec, 16)
            for n in range(6):
                load_weight(n)
            load_x(1, 0)
            for n in range(6, 9):
                load_weight(n)

            def step(t, par, j, more):
                if more:
                    sp.wait_ge(x1_done, 4 * t)
                    load_x(1 - par, (j + par) * TB)
                sp.wait_ge(y_done, 4 * t)
                sp.dma_start(out_d[:, bass.ds((j + par - 1) * TB + (1 - par) * T // P, TB), :],
                             x1[:, 1 - par, :, :]).then_inc(s_stored[1 - par], 16)

            run(sp, lambda: None, step, lambda: None)
            sp.wait_ge(y_done, 4 * NT)
            sp.dma_start(out_d[:, NT * TB - TB:NT * TB, :], x1[:, 1, :, :]).then_inc(s_stored[1], 16)
            sp.wait_ge(s_stored[0], 16 * NT // 2)
            sp.wait_ge(s_stored[1], 16 * NT // 2)

        @block.tensor
        def _(pe):
            def three(dst, pairs, first=True, last=True):
                for n, (a_hi, a_lo, b_hi, b_lo) in enumerate(pairs):
                    pe.matmul(dst, a_hi, b_hi, start=first and n == 0, stop=False)
                    pe.matmul(dst, a_hi, b_lo, start=False, stop=False)
                    mm = pe.matmul(dst, a_lo, b_hi, start=False, stop=last and n == len(pairs) - 1)
                return mm

            def cols(w, c, m):
                return w[:, c, m * P:(m + 1) * P]

            def proj(t):
                pe.wait_ge(xlo_done, 4 * t + 4)
                pe.wait_ge(delta_done, t)
                three(z_bank[:, :], [(wdelta_hi[:, c, :], wdelta_lo[:, c, :], xT_hi[:, c, :], xT_lo[:, c, :])
                                     for c in range(CH)]).then_inc(z_ready, 1)
                pe.wait_ge(bbar_done, t)
                three(b_bank[:, :], [(wb_hi[:, c, :], wb_lo[:, c, :], xT_hi[:, c, :], xT_lo[:, c, :])
                                     for c in range(CH)]).then_inc(b_ready, 1)

            def att(t):
                for tb in range(TB):
                    if tb >= 2:
                        pe.wait_ge(u2_done, 4 * t + tb - 1)
                    dst = av_bank[tb % 2][:, :]
                    pe.matmul(dst, ones[:, :], bias_rows[:, :], start=True, stop=False)
                    three(dst, [(cols(xT_hi, c, tb), cols(xT_lo, c, tb), wd_hi[:, c, :], wd_lo[:, c, :])
                                for c in range(CH)], first=False, last=False)
                    if tb == 0:
                        pe.wait_ge(h_split, t + 1)
                    three(dst, [(h_hi[:, tb * P:(tb + 1) * P], h_lo[:, tb * P:(tb + 1) * P], wc_hi[:, :], wc_lo[:, :])],
                          first=False).then_inc(att_ready, 1)

            def t1(t, tb, after_t2=True):
                pe.wait_ge(xn_done, 4 * t + tb + 1)
                if tb >= 2:
                    pe.wait_ge(xlo_done, 4 * t + tb - 1)
                elif after_t2:
                    pe.wait_ge(evac_done, 4 * (t - 2) + 3 + tb)
                for c in range(CH):
                    mm = pe.transpose(tr_bank[tb % 2][:, c * P:(c + 1) * P], xn[:, tb % 2, c * P:(c + 1) * P], ident[:, :])
                mm.then_inc(t1_ready, 1)

            def t2(t, tb, after_t1):
                pe.wait_ge(x1n_done, 4 * t + tb + 1)
                if tb >= 2:
                    pe.wait_ge(evac_done, 4 * t + tb - 1)
                elif after_t1:
                    pe.wait_ge(xlo_done, 4 * t + 7 + tb)
                else:
                    pe.wait_ge(evac_done, 4 * t - 1 + tb)
                for c in range(CH):
                    mm = pe.transpose(tr_bank[tb % 2][:, c * P:(c + 1) * P], x1n[:, tb, c * P:(c + 1) * P], ident[:, :])
                mm.then_inc(t2_ready, 1)

            def k_product(u):
                pe.wait_ge(mix_split, 8 * u + 4)
                pe.wait_ge(w_done, 4 * u)
                for f in range(CH):
                    if f >= 2:
                        pe.wait_ge(relu_done, 4 * u + f - 1)
                    three(kr_bank[f % 2][:, :], [(cols(wk_hi, c, f), cols(wk_lo, c, f), mix_hi[:, c, :], mix_lo[:, c, :])
                                                 for c in range(CH)]).then_inc(k_ready, 1)

            def r_product(u, tb):
                if tb == 0:
                    pe.wait_ge(mix_split, 8 * u + 8)
                if tb < 2:
                    pe.wait_ge(relu_done, 4 * u + 3 + tb)
                else:
                    pe.wait_ge(sig_done, 4 * u + tb - 1)
                three(kr_bank[tb % 2][:, :], [(cols(mix_hi, c, tb), cols(mix_lo, c, tb), wr_hi[:, c, :], wr_lo[:, c, :])
                                              for c in range(CH)]).then_inc(r_ready, 1)

            def v_product(u, tb, after_att=True):
                if tb == 0:
                    pe.wait_ge(ka_split, 4 * u + 4)
                if tb >= 2:
                    pe.wait_ge(w_done, 4 * u + tb - 1)
                elif after_att:
                    pe.wait_ge(u2_done, 4 * u + 7 + tb)
                three(av_bank[tb % 2][:, :], [(cols(ka_hi, f, tb), cols(ka_lo, f, tb), wv_hi[:, f, :], wv_lo[:, f, :])
                                              for f in range(CH)]).then_inc(v_ready, 1)

            def first():
                pe.wait_ge(s_ident, 2)
                for tb in range(TB):
                    t1(0, tb, after_t2=False)
                pe.wait_ge(s_wsplit, 2)
                proj(0)
                pe.wait_ge(s_wsplit, 5)
                pe.wait_ge(s_const, CONSTANTS)
                att(0)
                for tb in range(TB):
                    t1(1, tb, after_t2=False)
                for tb in range(TB):
                    t2(0, tb, after_t1=True)
                pe.wait_ge(s_wsplit, 8)

            def step(t, par, j, more):
                u = t - 1
                proj(t)
                k_product(u)
                att(t)
                if more:
                    t1(t + 1, 0)
                    t1(t + 1, 1)
                r_product(u, 0)
                if more:
                    t1(t + 1, 2)
                r_product(u, 1)
                if more:
                    t1(t + 1, 3)
                r_product(u, 2)
                t2(t, 0, more)
                t2(t, 1, more)
                r_product(u, 3)
                t2(t, 2, more)
                t2(t, 3, more)
                for tb in range(TB):
                    v_product(u, tb)

            def last():
                u = NT - 1
                k_product(u)
                for tb in range(TB):
                    r_product(u, tb)
                for tb in range(TB):
                    v_product(u, tb, after_att=False)

            run(pe, first, step, last)

        @block.scalar
        def _(act):
            def softplus_exp_log(t):
                act.preload_act_table_set("natural_log_exp_and_others")
                act.wait_ge(zc_done, t + 1)
                nc.scalar.activation(soft[:, :], soft[:, :], ACT.Exp).then_inc(e_done, 1)
                act.wait_ge(e_done, t + 1)
                nc.scalar.activation(soft[:, :], soft[:, :], ACT.Ln, bias=1.0).then_inc(l_done, 1)

            def decay(t):
                act.wait_ge(dc_done, t + 1)
                nc.scalar.activation(soft[:, :], soft[:, :], ACT.Exp).then_inc(g_done, 1)

            def k_square(u, f):
                if f == 0:
                    act.wait_ge(ka_split, 4 * u)
                if f >= 2:
                    act.wait_ge(ka_split, 4 * u + f - 1)
                act.wait_ge(k_ready, 4 * u + f + 1)
                nc.scalar.activation(relu[:, f % 2, :], kr_bank[f % 2][:, :], ACT.Relu).then_inc(relu_done, 1)
                act.wait_ge(relu_done, 4 * u + f + 1)
                nc.scalar.activation(ka_hi[:, f, :], relu[:, f % 2, :], ACT.Square).then_inc(kahi_done, 1)

            def normalise(out_ap, in_ap, kind, tb):
                return nc.scalar.activation(out_ap, in_ap, ACT.Identity, bias=nmr[:, kind, tb:tb + 1],
                                            scale=rstd[:, kind, tb:tb + 1])

            def xn_block(t, tb):
                if tb == 0:
                    act.wait_ge(nm[0], t + 1)
                if tb >= 2:
                    act.wait_ge(t1_ready, 4 * t + tb - 1)
                normalise(xn[:, tb % 2, :], x[:, t_parity[0], tb, :], 0, tb).then_inc(xn_done, 1)

            def xT_hi_block(t, tb):
                act.wait_ge(t1_ready, 4 * t + tb + 1)
                nc.scalar.copy(xT_hi[:, :, tb * P:(tb + 1) * P],
                               tr_bank[tb % 2][:, :].rearrange("p (c k) -> p c k", c=CH)).then_inc(xhi_done, 1)

            def u2_block(t, par, j, tb):
                if tb == 0:
                    act.wait_ge(s_stored[par], 16 * j)
                act.wait_ge(nm[1], 4 * t + tb + 1)
                normalise(x1[:, par, tb, :], av_bank[tb % 2][:, :], 1, tb).then_inc(u2_done, 1)

            def x1n_block(t, par, tb):
                act.wait_ge(nm[2], 4 * t + tb + 1)
                normalise(x1n[:, tb, :], x1[:, par, tb, :], 2, tb).then_inc(x1n_done, 1)

            def sigmoid(u, tb):
                if tb == 0:
                    act.wait_ge(y_done, 4 * u)
                act.wait_ge(r_ready, 4 * u + tb + 1)
                nc.scalar.activation(sig[:, tb, :], kr_bank[tb % 2][:, :], ACT.Sigmoid).then_inc(sig_done, 1)

            def x1T_block(t, par, tb):
                psum = tr_bank[tb % 2][:, :].rearrange("p (c k) -> p c k", c=CH)
                if tb == 0:
                    act.wait_ge(mixf_done, 8 * t)
                    nc.scalar.copy(x1T[:, :, 0], x1T_carry[:, par, :]).then_inc(x1c_done, 1)
                act.wait_ge(t2_ready, 4 * t + tb + 1)
                if tb == TB - 1:
                    nc.scalar.copy(x1T_carry[:, par, :], psum[:, :, P - 1]).then_inc(x1c_done, 1)
                nc.scalar.copy(x1T[:, :, 1 + tb * P:1 + (tb + 1) * P], psum).then_inc(evac_done, 1)

            def u4_block(u, tb):
                act.wait_ge(nm[3], 4 * u + tb + 1)
                normalise(sig[:, tb, :], sig[:, tb, :], 3, tb).then_inc(u4_done, 1)

            t_parity = [0]

            def first():
                act.preload_act_table_set("natural_log_exp_and_others")
                act.wait_ge(s_asoft, 1)
                nc.scalar.activation(a_tmp[:, 0:1], a_tmp[:, 0:1], ACT.Exp).then_inc(s_asoft, 1)
                act.wait_ge(s_asoft, 2)
                nc.scalar.activation(a_tmp[:, 0:1], a_tmp[:, 0:1], ACT.Ln, bias=1.0).then_inc(s_asoft, 1)
                act.wait_ge(s_const, CONSTANTS)
                xn_block(0, 0)
                xn_block(0, 1)
                for tb in range(TB):
                    xT_hi_block(0, tb)
                    if tb < 2:
                        xn_block(0, tb + 2)
                softplus_exp_log(0)
                decay(0)
                t_parity[0] = 1
                xn_block(1, 0)
                xn_block(1, 1)
                u2_block(0, 0, 0, 0)
                u2_block(0, 0, 0, 1)
                x1n_block(0, 0, 0)
                u2_block(0, 0, 0, 2)
                x1n_block(0, 0, 1)
                u2_block(0, 0, 0, 3)
                x1n_block(0, 0, 2)
                x1n_block(0, 0, 3)
                for tb in range(TB):
                    xT_hi_block(1, tb)
                    if tb < 2:
                        xn_block(1, tb + 2)
                for tb in range(TB):
                    x1T_block(0, 0, tb)

            def step(t, par, j, more):
                u = t - 1
                t_parity[0] = 1 - par
                softplus_exp_log(t)
                k_square(u, 0)
                decay(t)
                for f in range(1, CH):
                    k_square(u, f)
                if more:
                    xn_block(t + 1, 0)
                    xn_block(t + 1, 1)
                u2_block(t, par, j, 0)
                u2_block(t, par, j, 1)
                x1n_block(t, par, 0)
                u2_block(t, par, j, 2)
                x1n_block(t, par, 1)
                u2_block(t, par, j, 3)
                x1n_block(t, par, 2)
                if more:
                    xT_hi_block(t + 1, 0)
                    xn_block(t + 1, 2)
                x1n_block(t, par, 3)
                if more:
                    xT_hi_block(t + 1, 1)
                    xn_block(t + 1, 3)
                sigmoid(u, 0)
                if more:
                    xT_hi_block(t + 1, 2)
                sigmoid(u, 1)
                if more:
                    xT_hi_block(t + 1, 3)
                sigmoid(u, 2)
                x1T_block(t, par, 0)
                x1T_block(t, par, 1)
                sigmoid(u, 3)
                x1T_block(t, par, 2)
                x1T_block(t, par, 3)
                for tb in range(TB):
                    u4_block(u, tb)

            def last():
                u = NT - 1
                for f in range(CH):
                    k_square(u, f)
                for tb in range(TB):
                    sigmoid(u, tb)
                for tb in range(TB):
                    u4_block(u, tb)

            run(act, first, step, last)

        @block.vector
        def _(dve):
            v = nc.vector

            def norm_stats(kind, tb, in_ap, bn, done, n):
                v.bn_stats(stats[:, kind, tb % 2, :], in_ap).then_inc(bn, 1)
                dve.drain()
                v.bn_aggr(mv[:, kind, tb, :], stats[:, kind, tb % 2, :]).then_inc(done, 1)

            def ln1_stats(t, par, j):
                dve.wait_ge(s_xl[par], 16 * (j + 1))
                for tb in range(TB):
                    norm_stats(0, tb, x[:, par, tb, :], bn1, mv1, 4 * t + tb)

            def xT_lo_block(t, tb):
                dve.wait_ge(xhi_done, 4 * t + tb + 1)
                ks = slice(tb * P, (tb + 1) * P)
                v.tensor_tensor(xT_lo[:, :, ks], tr_bank[tb % 2][:, :].rearrange("p (c k) -> p c k", c=CH),
                                xT_hi[:, :, ks].bitcast(F32), ALU.subtract).then_inc(xlo_done, 1)

            def softplus_clamp(t):
                dve.wait_ge(z_ready, t + 1)
                v.tensor_scalar(soft[:, :], z_bank[:, :], bdelta_v, SOFTPLUS_MAX, ALU.add, ALU.min).then_inc(zc_done, 1)

            def log_decay(t, par):
                dve.wait_ge(l_done, t + 1)
                v.scalar_tensor_tensor(delta[:, :], z_bank[:, :], bdelta_v, soft[:, :], ALU.add, ALU.max).then_inc(delta_done, 1)
                dve.wait_ge(delta_done, t + 1)
                v.tensor_scalar(soft[:, :], delta[:, :], a_neg[:, 0:1], None, ALU.mult).then_inc(a_done, 1)
                v.tensor_copy(cum[:, 0:1], cum_carry[:, par:par + 1]).then_inc(col0_done, 1)
                dve.wait_ge(a_done, t + 1)
                dve.wait_ge(col0_done, t + 1)
                v.tensor_tensor_scan(cum[:, 1:], soft[:, :], soft[:, :], cum[:, 0:1], ALU.add, ALU.bypass).then_inc(cum_done, 1)
                dve.wait_ge(cum_done, t + 1)
                v.tensor_copy(cum_carry[:, par:par + 1], cum[:, TILE:TILE + 1]).then_inc(cumc_done, 1)
                dve.wait_ge(cumc_done, t + 1)
                v.tensor_scalar(cum[:, :], cum[:, :], -CLIP, CLIP, ALU.max, ALU.min).then_inc(c_done, 1)
                dve.wait_ge(c_done, t + 1)
                v.tensor_tensor(soft[:, :], cum[:, 1:], cum[:, 0:TILE], ALU.subtract).then_inc(dc_done, 1)
                dve.wait_ge(b_ready, t + 1)
                v.scalar_tensor_tensor(bbar[:, :], b_bank[:, :], bb_v, delta[:, :], ALU.add, ALU.mult).then_inc(bbar_done, 1)

            def recurrence(t, par):
                dve.wait_ge(bbar_done, t + 1)
                dve.wait_ge(g_done, t + 1)
                v.tensor_tensor_scan(delta[:, :], bbar[:, :], soft[:, :], h_carry[:, par:par + 1], ALU.add, ALU.mult).then_inc(h_done, 1)
                dve.wait_ge(h_done, t + 1)
                dve.wait_ge(att_ready, 4 * t)
                v.tensor_copy(h_hi[:, :], delta[:, :]).then_inc(hhi_done, 1)
                v.tensor_copy(h_carry[:, par:par + 1], delta[:, TILE - 1:TILE])
                dve.wait_ge(hhi_done, t + 1)
                v.tensor_tensor(h_lo[:, :], delta[:, :], h_hi[:, :].bitcast(F32), ALU.subtract).then_inc(h_split, 1)

            def k_lo(u, f):
                dve.wait_ge(kahi_done, 4 * u + f + 1)
                v.tensor_tensor(relu[:, f % 2, :], relu[:, f % 2, :], relu[:, f % 2, :], ALU.mult).then_inc(sq_done, 1)
                dve.wait_ge(sq_done, 4 * u + f + 1)
                v.tensor_tensor(ka_lo[:, f, :], relu[:, f % 2, :], ka_hi[:, f, :].bitcast(F32), ALU.subtract).then_inc(ka_split, 1)

            def mix(u, for_r, c):
                n = 8 * u + 4 * for_r + c
                mu = (mu_r if for_r else mu_k)[:, c:c + 1]
                dve.wait_ge(diff_done, n + 1)
                f = mixf[:, c % 2, :]
                v.scalar_tensor_tensor(f, f, mu, x1T[:, c, 0:TILE], ALU.mult, ALU.add).then_inc(mixf_done, 1)
                dve.wait_ge(mixf_done, n + 1)
                if c == 0:
                    dve.wait_ge(k_ready if for_r else r_ready, 4 * u + 4 * for_r)
                v.tensor_copy(mix_hi[:, c, :], f).then_inc(mixhi_done, 1)
                dve.wait_ge(mixhi_done, n + 1)
                v.tensor_tensor(mix_lo[:, c, :], f, mix_hi[:, c, :].bitcast(F32), ALU.subtract).then_inc(mix_split, 1)

            def ln2_stats(t, tb):
                dve.wait_ge(att_ready, 4 * t + tb + 1)
                norm_stats(1, tb, av_bank[tb % 2][:, :], bn2, mv2, 4 * t + tb)

            def ln3_stats(t, par, tb):
                dve.wait_ge(x1_done, 4 * t + tb + 1)
                norm_stats(2, tb, x1[:, par, tb, :], bn3, mv3, 4 * t + tb)

            def gate(u, tb):
                dve.wait_ge(sig_done, 4 * u + tb + 1)
                dve.wait_ge(v_ready, 4 * u + tb + 1)
                v.tensor_tensor(sig[:, tb, :], av_bank[tb % 2][:, :], sig[:, tb, :], ALU.mult).then_inc(w_done, 1)
                dve.wait_ge(w_done, 4 * u + tb + 1)
                norm_stats(3, tb, sig[:, tb, :], bn4, mv4, 4 * u + tb)

            def split(n, hi, lo):
                stage = STAGED[n]
                dve.wait_ge(s_w[n], 16)
                v.tensor_copy(hi, stage).then_inc(s_whi, 1)
                dve.wait_ge(s_whi, SPLITS.index(n) + 1)
                v.tensor_tensor(lo, stage, hi.bitcast(F32), ALU.subtract).then_inc(s_wsplit, 1)

            def first():
                v.memset(cum_carry[:, :], 0.0).then_inc(s_const, 1)
                v.memset(h_carry[:, :], 0.0).then_inc(s_const, 1)
                v.memset(x1T_carry[:, :, :], 0.0).then_inc(s_const, 1)
                v.memset(mhalf[:, :], -0.5).then_inc(s_const, 1)
                v.memset(epsilon[:, :], EPS).then_inc(s_const, 1)
                v.memset(minus1[:, :], -1.0).then_inc(s_const, 1)
                v.memset(bbar[:, 0:P], 1.0).then_inc(s_const, 1)
                dve.wait_ge(s_const, 7)
                v.tensor_copy(ones[:, :], bbar[:, 0:P]).then_inc(s_const, 1)
                dve.wait_ge(s_vec, 16)
                v.tensor_scalar(a_tmp[:, 0:1], A_v, SOFTPLUS_MAX, None, ALU.min).then_inc(s_asoft, 1)
                dve.wait_ge(s_asoft, 3)
                v.tensor_scalar(a_neg[:, 0:1], a_tmp[:, 0:1], A_v, -1.0, ALU.max, ALU.mult).then_inc(s_const, 1)
                dve.wait_ge(s_const, CONSTANTS)
                ln1_stats(0, 0, 0)
                split(0, wdelta_hi[:, :, :].rearrange("p c n -> p (c n)"), wdelta_lo[:, :, :].rearrange("p c n -> p (c n)"))
                split(1, wb_hi[:, :, :].rearrange("p c n -> p (c n)"), wb_lo[:, :, :].rearrange("p c n -> p (c n)"))
                for tb in range(TB):
                    xT_lo_block(0, tb)
                split(2, wd_hi[:, :, :], wd_lo[:, :, :])
                split(3, wc_hi[:, :], wc_lo[:, :])
                dve.wait_ge(s_w[4], 16)
                dve.wait_ge(s_w[5], 16)
                b_sum = STAGED[4]
                v.tensor_tensor(b_sum, STAGED[4], STAGED[5], ALU.add).then_inc(s_bias, 1)
                dve.wait_ge(s_bias, 1)
                v.tensor_scalar(b_sum, b_sum, 2.0 / P, None, ALU.mult).then_inc(s_bias, 1)
                dve.wait_ge(s_bias, 2)
                v.tensor_copy(bias_rows[:, :], b_sum).then_inc(s_bias, 1)
                dve.wait_ge(s_bias, 3)
                v.tensor_tensor(bias_rows[P // 2:, :], b_sum[P // 2:, :], bias_rows[P // 2:, :].bitcast(F32),
                                ALU.subtract).then_inc(s_wsplit, 1)
                softplus_clamp(0)
                ln1_stats(1, 1, 0)
                log_decay(0, 0)
                recurrence(0, 0)
                ln2_stats(0, 0)
                ln2_stats(0, 1)
                ln3_stats(0, 0, 0)
                ln2_stats(0, 2)
                ln3_stats(0, 0, 1)
                ln2_stats(0, 3)
                ln3_stats(0, 0, 2)
                ln3_stats(0, 0, 3)
                for tb in range(TB):
                    xT_lo_block(1, tb)
                split(6, wk_hi[:, :, :], wk_lo[:, :, :])
                split(7, wr_hi[:, :, :], wr_lo[:, :, :])
                split(8, wv_hi[:, :, :], wv_lo[:, :, :])
                for c in range(CH):
                    mix(0, 0, c)

            def step(t, par, j, more):
                u = t - 1
                softplus_clamp(t)
                if more:
                    ln1_stats(t + 1, 1 - par, j + par)
                log_decay(t, par)
                k_lo(u, 0)
                recurrence(t, par)
                for f in range(1, CH):
                    k_lo(u, f)
                mix(u, 1, 0)
                ln2_stats(t, 0)
                mix(u, 1, 1)
                ln2_stats(t, 1)
                ln3_stats(t, par, 0)
                mix(u, 1, 2)
                ln2_stats(t, 2)
                ln3_stats(t, par, 1)
                mix(u, 1, 3)
                ln2_stats(t, 3)
                ln3_stats(t, par, 2)
                ln3_stats(t, par, 3)
                if more:
                    for tb in range(TB):
                        xT_lo_block(t + 1, tb)
                mix(t, 0, 0)
                mix(t, 0, 1)
                gate(u, 0)
                mix(t, 0, 2)
                gate(u, 1)
                mix(t, 0, 3)
                gate(u, 2)
                gate(u, 3)

            def last():
                u = NT - 1
                for f in range(CH):
                    k_lo(u, f)
                for c in range(CH):
                    mix(u, 1, c)
                for tb in range(TB):
                    gate(u, tb)

            run(dve, first, step, last)

        @block.gpsimd
        def _(pool):
            g = nc.gpsimd

            def scales(kind, tb, blocks, ready, n_ready, n):
                s = slice(tb, tb + blocks)
                pool.wait_ge(ready, n_ready)
                g.tensor_tensor(vare[:, kind, s], mv[:, kind, s, 1], epsilon[:, 0:blocks], ALU.add).then_inc(ve[kind], 1)
                pool.wait_ge(ve[kind], n + 1)
                g.tensor_tensor(rstd[:, kind, s], vare[:, kind, s], mhalf[:, 0:blocks], ALU.pow).then_inc(rs[kind], 1)
                pool.wait_ge(rs[kind], n + 1)
                g.tensor_tensor(nmr[:, kind, s], mv[:, kind, s, 0], rstd[:, kind, s], ALU.mult).then_inc(nmp[kind], 1)
                pool.wait_ge(nmp[kind], n + 1)
                g.tensor_tensor(nmr[:, kind, s], nmr[:, kind, s], minus1[:, 0:blocks], ALU.mult).then_inc(nm[kind], 1)

            def x1_scales(t, tb):
                scales(1, tb, 1, mv2, 4 * t + tb + 1, 4 * t + tb)

            def x1_add(t, par, tb):
                pool.wait_ge(u2_done, 4 * t + tb + 1)
                g.tensor_tensor(x1[:, par, tb, :], x1[:, par, tb, :], x[:, par, tb, :], ALU.add).then_inc(x1_done, 1)

            def x1n_scales(t, tb):
                scales(2, tb, 1, mv3, 4 * t + tb + 1, 4 * t + tb)

            def y_scales(u, tb):
                scales(3, tb, 1, mv4, 4 * u + tb + 1, 4 * u + tb)

            def y_add(u, par, tb):
                pool.wait_ge(u4_done, 4 * u + tb + 1)
                g.tensor_tensor(x1[:, par, tb, :], x1[:, par, tb, :], sig[:, tb, :], ALU.add).then_inc(y_done, 1)

            def diff(u, for_r, c):
                n = 8 * u + 4 * for_r + c
                if not for_r and c == 0:
                    pool.wait_ge(evac_done, 4 * u + 4)
                    pool.wait_ge(mix_split, 8 * u)
                elif for_r or c >= 2:
                    pool.wait_ge(mix_split, n - 1)
                g.tensor_tensor(mixf[:, c % 2, :], x1T[:, c, 1:], x1T[:, c, 0:TILE], ALU.subtract).then_inc(diff_done, 1)

            def first():
                g.memset(ident[:, :], 0.0).then_inc(s_ident, 1)
                pool.wait_ge(s_ident, 1)
                g.affine_select(out=ident[:, :], in_=ident[:, :], compare_op=ALU.not_equal, fill=1.0, base=0,
                                pattern=[[-1, P]], channel_multiplier=1).then_inc(s_ident, 1)
                pool.wait_ge(s_const, CONSTANTS)
                scales(0, 0, TB, mv1, 4, 0)
                scales(0, 0, TB, mv1, 8, 1)
                x1_scales(0, 0)
                x1_add(0, 0, 0)
                x1_scales(0, 1)
                x1_add(0, 0, 1)
                x1n_scales(0, 0)
                x1_scales(0, 2)
                x1_add(0, 0, 2)
                x1n_scales(0, 1)
                x1_scales(0, 3)
                x1_add(0, 0, 3)
                x1n_scales(0, 2)
                x1n_scales(0, 3)
                pool.wait_ge(s_wsplit, 8)
                for c in range(CH):
                    diff(0, 0, c)

            def step(t, par, j, more):
                u = t - 1
                if more:
                    scales(0, 0, TB, mv1, 4 * t + 8, t + 1)
                diff(u, 1, 0)
                diff(u, 1, 1)
                x1_scales(t, 0)
                x1_add(t, par, 0)
                diff(u, 1, 2)
                x1_scales(t, 1)
                x1_add(t, par, 1)
                x1n_scales(t, 0)
                diff(u, 1, 3)
                x1_scales(t, 2)
                x1_add(t, par, 2)
                x1n_scales(t, 1)
                x1_scales(t, 3)
                x1_add(t, par, 3)
                x1n_scales(t, 2)
                x1n_scales(t, 3)
                for c in range(CH):
                    diff(t, 0, c)
                for tb in range(TB):
                    y_scales(u, tb)
                    y_add(u, 1 - par, tb)

            def last():
                u = NT - 1
                for c in range(CH):
                    diff(u, 1, c)
                for tb in range(TB):
                    y_scales(u, tb)
                    y_add(u, 1, tb)

            run(pool, first, step, last)


def kernel(**inputs):
    import numpy as _np
    import concourse.bacc as _bacc
    from concourse import mybir as _mybir
    from concourse.bass_utils import run_bass_kernel_spmd as _run

    a = {n.split("_", 2)[2]: _np.asarray(v) for n, v in inputs.items()}
    n_chunks = a["mu_r"].shape[0] // 128

    def chunked(w):
        return w.reshape(w.shape[0] // 128, 128, w.shape[1]).transpose(1, 0, 2)

    def rows(b):
        return _np.broadcast_to(b[None, :], (128, b.shape[0]))

    vectors = _np.concatenate([a["A"][:, None], a["bb"][:, None], a["bdelta"][:, None],
                               a["mu_r"].reshape(n_chunks, 128).T, a["mu_k"].reshape(n_chunks, 128).T], axis=1)
    arrays = {
        "x": a["x"], "vectors": vectors, "bc": rows(a["bc"]), "bd": rows(a["bd"]),
        "w_delta": chunked(a["Wdelta"]).reshape(128, -1), "w_b": chunked(a["Wb"]).reshape(128, -1),
        "w_c": a["Wc"], "w_d": chunked(a["Wd"]),
        "w_r": chunked(a["W_r"].T), "w_k": chunked(a["W_k"].T), "w_v": chunked(a["W_v"].T),
    }
    arrays = {k: _np.ascontiguousarray(v) for k, v in arrays.items()}
    nc = _bacc.Bacc("TRN2", target_bir_lowering=False, num_devices=1)
    args = {k: nc.dram_tensor(f"in_{k}_dram", v.shape, _mybir.dt.from_np(v.dtype), kind="ExternalInput").ap()
            for k, v in arrays.items()}
    out = nc.dram_tensor("out_dram", a["x"].shape, _mybir.dt.float32, kind="ExternalOutput").ap()
    state_space_mixer_and_channel_mixer(nc, args["x"], args["vectors"], args["bc"], args["bd"], args["w_delta"], args["w_b"],
                                        args["w_c"], args["w_d"], args["w_r"], args["w_k"], args["w_v"], out)
    r = _run(nc, [{f"in_{k}_dram": v for k, v in arrays.items()}], core_ids=[0])
    return r.results[0]["out_dram"]
```

```python
from contextlib import ExitStack

import concourse.bass as bass
from concourse import mybir

ALU = mybir.AluOpType
ACT = mybir.ActivationFunctionType
F32 = mybir.dt.float32
F32R = mybir.dt.float32r

P = 128
TILE = 512
TB = TILE // P
EPS = 1e-5
CLIP = 20.0
SOFTPLUS_MAX = 30.0


def state_space_mixer_and_channel_mixer(nc, x_in, vectors, bc, bd, w_delta, w_b, w_c, w_d, w_r, w_k, w_v, out):
    NB, T, DM = x_in.shape
    DH = w_c.shape[0]
    CH = DM // P
    NT = NB * T // TILE
    assert NB == 2 and DH == P and DM == 512 and NT % 2 == 0

    x_d = x_in.rearrange("b (n p) d -> p (b n) d", p=P)
    out_d = out.rearrange("b (n p) d -> p (b n) d", p=P)

    with ExitStack() as ctx:
        def sb(name, shape, dt=F32):
            return ctx.enter_context(nc.sbuf_tensor(name, shape, dt))

        def bank(name):
            return ctx.enter_context(nc.psum_tensor(name, [P, 512], F32))

        def sem(name):
            return ctx.enter_context(nc.semaphore(name))

        wdelta_hi, wdelta_lo = sb("wdelta_hi", [P, CH, DH], F32R), sb("wdelta_lo", [P, CH, DH], F32R)
        wb_hi, wb_lo = sb("wb_hi", [P, CH, DH], F32R), sb("wb_lo", [P, CH, DH], F32R)
        wc_hi, wc_lo = sb("wc_hi", [P, DM], F32R), sb("wc_lo", [P, DM], F32R)
        wd_hi, wd_lo = sb("wd_hi", [P, CH, DM], F32R), sb("wd_lo", [P, CH, DM], F32R)
        wr_hi, wr_lo = sb("wr_hi", [P, CH, DM], F32R), sb("wr_lo", [P, CH, DM], F32R)
        wk_hi, wk_lo = sb("wk_hi", [P, CH, DM], F32R), sb("wk_lo", [P, CH, DM], F32R)
        wv_hi, wv_lo = sb("wv_hi", [P, CH, DM], F32R), sb("wv_lo", [P, CH, DM], F32R)
        bias_rows = sb("bias_rows", [P, DM], F32R)
        ones = sb("ones", [P, P], F32R)
        ident = sb("ident", [P, P])
        vecs = sb("vecs", [P, vectors.shape[1]])
        x = sb("x", [P, 2, TB, DM])
        x1 = sb("x1", [P, 2, TB, DM])
        xn = sb("xn", [P, TB, DM])
        xT_hi, xT_lo = sb("xT_hi", [P, CH, TILE], F32R), sb("xT_lo", [P, CH, TILE], F32R)
        x1n = sb("x1n", [P, TB, DM])
        x1T = sb("x1T", [P, CH, TILE + 1])
        mix_hi, mix_lo = sb("mix_hi", [P, CH, TILE], F32R), sb("mix_lo", [P, CH, TILE], F32R)
        ka_hi, ka_lo = sb("ka_hi", [P, CH, TILE], F32R), sb("ka_lo", [P, CH, TILE], F32R)
        sig = sb("sig", [P, TB, DM])
        relu = sb("relu", [P, 2, TILE])
        mixf = sb("mixf", [P, CH, TILE])
        soft = sb("soft", [P, TILE])
        delta = sb("delta", [P, TILE])
        bbar = sb("bbar", [P, TILE])
        cum = sb("cum", [P, TILE + 1])
        h_hi, h_lo = sb("h_hi", [P, TILE], F32R), sb("h_lo", [P, TILE], F32R)
        smalls = sb("smalls", [P, 4 * 2 * 6 + 4 * TB * 5 + 3 * TB + 2 * CH + 2 + 2 * NB + NB * CH])
        taken = [0]

        def small(*shape):
            n = 1
            for k in shape:
                n *= k
            part = smalls[:, taken[0]:taken[0] + n]
            taken[0] += n
            names = " ".join("abc"[:len(shape)])
            return part.rearrange(f"p ({names}) -> p {names}", **dict(zip("abc", shape))) if len(shape) > 1 else part

        stats = small(4, 2, 6)
        mv = small(4, TB, 2)
        vare, rstd, nmr = small(4, TB), small(4, TB), small(4, TB)
        mhalf, epsilon, minus1 = small(TB), small(TB), small(TB)
        nmu = small(2 * CH)
        a_neg, a_tmp = small(1), small(1)
        cum_carry, h_carry = small(NB), small(NB)
        x1T_carry = small(NB, CH)

        A_v, bb_v, bdelta_v = vecs[:, 0:1], vecs[:, 1:2], vecs[:, 2:3]
        mu_r, mu_k = vecs[:, 3:3 + CH], vecs[:, 3 + CH:3 + 2 * CH]
        nmu_r, nmu_k = nmu[:, 0:CH], nmu[:, CH:2 * CH]

        kr_bank = [bank("kr0"), bank("kr1")]
        z_bank, b_bank = bank("zb"), bank("bb")
        av_bank = [bank("av0"), bank("av1"), z_bank, b_bank]
        tr_bank = [bank("tr0"), bank("tr1")]

        s_vec, s_w = sem("vectors_loaded"), [sem(f"weight{i}_loaded") for i in range(9)]
        s_stored = [sem("stored_even"), sem("stored_odd")]
        s_ident, s_const, s_asoft = sem("ident_ready"), sem("constants_ready"), sem("a_softplus")
        s_wsplit, s_whi, s_bias = sem("weights_split"), sem("weight_hi"), sem("bias_rows")
        nmp = [sem(f"ln{i + 1}_mean_rstd") for i in range(4)]
        s_xl = [sem("x_loaded_even"), sem("x_loaded_odd")]
        z_ready, b_ready = sem("z_ready"), sem("b_ready")
        k_ready, att_ready, t1_ready = sem("k_ready"), sem("att_ready"), sem("t1_ready")
        r_ready, t2_ready, v_ready = sem("r_ready"), sem("t2_ready"), sem("v_ready")
        zc_done, e_done, l_done = sem("z_clamped"), sem("exp_done"), sem("log_done")
        delta_done, a_done, cum_done, cumc_done = sem("delta_done"), sem("a_done"), sem("cum_done"), sem("cum_carried")
        c_done, dc_done, g_done, bbar_done = sem("clip_done"), sem("step_done"), sem("decay_done"), sem("bbar_done")
        col0_done, h_done, hhi_done, h_split = sem("cum_col0"), sem("h_done"), sem("h_hi_done"), sem("h_split")
        relu_done, kahi_done, sq_done, ka_split = sem("relu_done"), sem("ka_hi_done"), sem("square_done"), sem("ka_split")
        bn1, mv1, bn2, mv2 = sem("bn1"), sem("mv1"), sem("bn2"), sem("mv2")
        bn3, mv3, bn4, mv4 = sem("bn3"), sem("mv3"), sem("bn4"), sem("mv4")
        rs = [sem(f"ln{i + 1}_rstd") for i in range(4)]
        ve = [sem(f"ln{i + 1}_vare") for i in range(4)]
        nm = [sem(f"ln{i + 1}_scales") for i in range(4)]
        xn_done, xhi_done, xlo_done = sem("xn_done"), sem("xT_hi_done"), sem("xT_lo_done")
        u2_done, x1_done, x1n_done, evac_done = sem("u2_done"), sem("x1_done"), sem("x1n_done"), sem("x1T_done")
        x1c_done = sem("x1T_col0")
        prev_done, mixf_done, mixhi_done, mix_split = sem("prev_scaled"), sem("mixf_done"), sem("mix_hi_done"), sem("mix_split")
        sig_done, w_done, u4_done, y_done = sem("sig_done"), sem("w_done"), sem("u4_done"), sem("y_done")

        block = ctx.enter_context(nc.Block())

        def run(eng, first, step, last):
            first()
            step(1, 1, 0, True)
            with eng.Fori(1, NT // 2 - 1) as i:
                step(2 * i, 0, i, True)
                step(2 * i + 1, 1, i, True)
            step(NT - 2, 0, NT // 2 - 1, eng is not nc.sync)
            step(NT - 1, 1, NT // 2 - 1, False)
            last()

        WEIGHTS = [(w_delta, x1n[:, 0, :]), (w_b, x1n[:, 1, :]), (w_d, x1[:, 0, :, :]), (w_c, x1n[:, 2, :]),
                   (bc, x1n[:, 3, :]), (bd, soft[:, :]), (w_k, x1[:, 1, :, :]), (w_r, sig[:, :, :]), (w_v, mixf[:, :, :])]
        STAGED = [s for _, s in WEIGHTS]
        SPLITS = [0, 1, 2, 3, 6, 7, 8]
        CONSTANTS = 10
        V_ORDER = [2, 3, 0, 1]

        @block.sync
        def _(sp):
            def load_x(par, block):
                sp.dma_start(x[:, par, :, :], x_d[:, bass.ds(block + par * T // P, TB), :]).then_inc(s_xl[par], 16)

            def load_weight(n):
                src, dst = WEIGHTS[n]
                sp.dma_start(dst, src).then_inc(s_w[n], 16)

            load_x(0, 0)
            sp.dma_start(vecs[:, :], vectors).then_inc(s_vec, 16)
            for n in range(6):
                load_weight(n)
            load_x(1, 0)
            for n in range(6, 9):
                load_weight(n)

            def step(t, par, j, more):
                if more:
                    sp.wait_ge(x1_done, 4 * t + 4)
                    load_x(par, (j + 1) * TB)
                sp.wait_ge(y_done, 4 * t)
                sp.dma_start(out_d[:, bass.ds((j + par - 1) * TB + (1 - par) * T // P, TB), :],
                             x1[:, 1 - par, :, :]).then_inc(s_stored[1 - par], 16)

            def first():
                sp.wait_ge(x1_done, 4)
                load_x(0, TB)

            run(sp, first, step, lambda: None)
            sp.wait_ge(y_done, 4 * NT)
            sp.dma_start(out_d[:, NT * TB - TB:NT * TB, :], x1[:, 1, :, :]).then_inc(s_stored[1], 16)
            sp.wait_ge(s_stored[0], 16 * NT // 2)
            sp.wait_ge(s_stored[1], 16 * NT // 2)

        @block.tensor
        def _(pe):
            def three(dst, pairs, first=True, last=True):
                for n, (a_hi, a_lo, b_hi, b_lo) in enumerate(pairs):
                    pe.matmul(dst, a_hi, b_hi, start=first and n == 0, stop=False)
                    pe.matmul(dst, a_hi, b_lo, start=False, stop=False)
                    mm = pe.matmul(dst, a_lo, b_hi, start=False, stop=last and n == len(pairs) - 1)
                return mm

            def cols(w, c, m):
                return w[:, c, m * P:(m + 1) * P]

            def proj(t, z_free, b_free):
                pe.wait_ge(xlo_done, 4 * t + 4)
                if z_free is not None:
                    pe.wait_ge(*z_free)
                three(z_bank[:, :], [(wdelta_hi[:, c, :], wdelta_lo[:, c, :], xT_hi[:, c, :], xT_lo[:, c, :])
                                     for c in range(CH)]).then_inc(z_ready, 1)
                if b_free is not None:
                    pe.wait_ge(*b_free)
                three(b_bank[:, :], [(wb_hi[:, c, :], wb_lo[:, c, :], xT_hi[:, c, :], xT_lo[:, c, :])
                                     for c in range(CH)]).then_inc(b_ready, 1)

            def att(t, t1_next=True):
                for tb in range(TB):
                    dst = av_bank[tb][:, :]
                    pe.matmul(dst, ones[:, :], bias_rows[:, :], start=True, stop=False)
                    three(dst, [(cols(xT_hi, c, tb), cols(xT_lo, c, tb), wd_hi[:, c, :], wd_lo[:, c, :])
                                for c in range(CH)], first=False, last=False)
                    if tb == 0:
                        pe.wait_ge(h_split, t + 1)
                    three(dst, [(h_hi[:, tb * P:(tb + 1) * P], h_lo[:, tb * P:(tb + 1) * P], wc_hi[:, :], wc_lo[:, :])],
                          first=False).then_inc(att_ready, 1)
                    if t1_next:
                        t1(t + 1, tb, after_t2=not isinstance(t, int) or t > 0)

            def t1(t, tb, after_t2=True):
                pe.wait_ge(xn_done, 4 * t + tb + 1)
                if tb >= 2:
                    pe.wait_ge(xlo_done, 4 * t + tb - 1)
                elif after_t2:
                    pe.wait_ge(evac_done, 4 * (t - 2) + 3 + tb)
                for c in range(CH):
                    mm = pe.transpose(tr_bank[tb % 2][:, c * P:(c + 1) * P], xn[:, tb, c * P:(c + 1) * P], ident[:, :])
                mm.then_inc(t1_ready, 1)

            def t2(t, tb, after_t1):
                pe.wait_ge(x1n_done, 4 * t + tb + 1)
                if tb >= 2:
                    pe.wait_ge(evac_done, 4 * t + tb - 1)
                elif after_t1:
                    pe.wait_ge(xlo_done, 4 * t + 7 + tb)
                else:
                    pe.wait_ge(evac_done, 4 * t - 1 + tb)
                for c in range(CH):
                    mm = pe.transpose(tr_bank[tb % 2][:, c * P:(c + 1) * P], x1n[:, tb, c * P:(c + 1) * P], ident[:, :])
                mm.then_inc(t2_ready, 1)

            def k_product(u):
                pe.wait_ge(mix_split, 8 * u + 4)
                pe.wait_ge(w_done, 4 * u)
                for f in range(CH):
                    if f >= 2:
                        pe.wait_ge(relu_done, 4 * u + f - 1)
                    three(kr_bank[f % 2][:, :], [(cols(wk_hi, c, f), cols(wk_lo, c, f), mix_hi[:, c, :], mix_lo[:, c, :])
                                                 for c in range(CH)]).then_inc(k_ready, 1)

            def r_product(u, tb):
                if tb == 0:
                    pe.wait_ge(mix_split, 8 * u + 8)
                if tb < 2:
                    pe.wait_ge(relu_done, 4 * u + 3 + tb)
                else:
                    pe.wait_ge(sig_done, 4 * u + tb - 1)
                three(kr_bank[tb % 2][:, :], [(cols(mix_hi, c, tb), cols(mix_lo, c, tb), wr_hi[:, c, :], wr_lo[:, c, :])
                                              for c in range(CH)]).then_inc(r_ready, 1)

            def v_product(u, tb, after_att=True):
                if tb == V_ORDER[0]:
                    pe.wait_ge(ka_split, 4 * u + 4)
                    if after_att:
                        pe.wait_ge(u2_done, 4 * u + 8)
                three(av_bank[tb][:, :], [(cols(ka_hi, f, tb), cols(ka_lo, f, tb), wv_hi[:, f, :], wv_lo[:, f, :])
                                              for f in range(CH)]).then_inc(v_ready, 1)

            def first():
                pe.wait_ge(s_ident, 2)
                for tb in range(TB):
                    t1(0, tb, after_t2=False)
                pe.wait_ge(s_wsplit, 2)
                proj(0, None, None)
                pe.wait_ge(s_wsplit, 5)
                pe.wait_ge(s_const, CONSTANTS)
                att(0)
                for tb in range(TB):
                    t2(0, tb, after_t1=True)
                pe.wait_ge(s_wsplit, 8)

            def step(t, par, j, more):
                u = t - 1
                if isinstance(t, int) and t == 1:
                    proj(t, (u2_done, 3), (u2_done, 4))
                else:
                    proj(t, (w_done, 4 * t - 7), (w_done, 4 * t - 6))
                k_product(u)
                att(t, t1_next=more)
                r_product(u, 0)
                r_product(u, 1)
                t2(t, 0, more)
                t2(t, 1, more)
                r_product(u, 2)
                r_product(u, 3)
                t2(t, 2, more)
                t2(t, 3, more)
                for tb in V_ORDER:
                    v_product(u, tb)

            def last():
                u = NT - 1
                k_product(u)
                for tb in range(TB):
                    r_product(u, tb)
                for tb in V_ORDER:
                    v_product(u, tb, after_att=False)

            run(pe, first, step, last)

        @block.scalar
        def _(act):
            def softplus_exp_log(t):
                act.preload_act_table_set("natural_log_exp_and_others")
                act.wait_ge(zc_done, t + 1)
                nc.scalar.activation(soft[:, :], soft[:, :], ACT.Exp).then_inc(e_done, 1)
                act.wait_ge(e_done, t + 1)
                nc.scalar.activation(soft[:, :], soft[:, :], ACT.Ln, bias=1.0).then_inc(l_done, 1)

            def decay(t):
                act.wait_ge(dc_done, t + 1)
                nc.scalar.activation(soft[:, :], soft[:, :], ACT.Exp).then_inc(g_done, 1)

            def k_square(u, f):
                if f == 0:
                    act.wait_ge(ka_split, 4 * u)
                if f >= 2:
                    act.wait_ge(ka_split, 4 * u + f - 1)
                act.wait_ge(k_ready, 4 * u + f + 1)
                nc.scalar.activation(relu[:, f % 2, :], kr_bank[f % 2][:, :], ACT.Relu).then_inc(relu_done, 1)
                act.wait_ge(relu_done, 4 * u + f + 1)
                nc.scalar.activation(ka_hi[:, f, :], relu[:, f % 2, :], ACT.Square).then_inc(kahi_done, 1)

            def normalise(out_ap, in_ap, kind, tb):
                return nc.scalar.activation(out_ap, in_ap, ACT.Identity, bias=nmr[:, kind, tb:tb + 1],
                                            scale=rstd[:, kind, tb:tb + 1])

            def xn_block(t, tb):
                if tb == 0:
                    act.wait_ge(nm[0], t + 1)
                normalise(xn[:, tb, :], x[:, t_parity[0], tb, :], 0, tb).then_inc(xn_done, 1)

            def xT_hi_block(t, tb):
                act.wait_ge(t1_ready, 4 * t + tb + 1)
                nc.scalar.copy(xT_hi[:, :, tb * P:(tb + 1) * P],
                               tr_bank[tb % 2][:, :].rearrange("p (c k) -> p c k", c=CH)).then_inc(xhi_done, 1)

            def u2_block(t, par, j, tb):
                if tb == 0:
                    act.wait_ge(s_stored[par], 16 * j)
                if tb % 2 == 0:
                    act.wait_ge(nm[1], 2 * t + tb // 2 + 1)
                normalise(x1[:, par, tb, :], av_bank[tb][:, :], 1, tb).then_inc(u2_done, 1)

            def sigmoid(u, tb):
                if tb == 0:
                    act.wait_ge(y_done, 4 * u)
                act.wait_ge(r_ready, 4 * u + tb + 1)
                nc.scalar.activation(sig[:, tb, :], kr_bank[tb % 2][:, :], ACT.Sigmoid).then_inc(sig_done, 1)

            def x1T_block(t, par, tb):
                psum = tr_bank[tb % 2][:, :].rearrange("p (c k) -> p c k", c=CH)
                if tb == 0:
                    act.wait_ge(mixf_done, 8 * t)
                    nc.scalar.copy(x1T[:, :, 0], x1T_carry[:, par, :]).then_inc(x1c_done, 1)
                act.wait_ge(t2_ready, 4 * t + tb + 1)
                if tb == TB - 1:
                    nc.scalar.copy(x1T_carry[:, par, :], psum[:, :, P - 1]).then_inc(x1c_done, 1)
                nc.scalar.copy(x1T[:, :, 1 + tb * P:1 + (tb + 1) * P], psum).then_inc(evac_done, 1)

            def scale_prev(u, for_r, c):
                if not for_r and c == 0:
                    act.wait_ge(evac_done, 4 * u + 4)
                    act.wait_ge(mix_split, 8 * u)
                elif for_r:
                    act.wait_ge(mix_split, 8 * u + c + 1)
                nc.scalar.mul(mixf[:, c, :], x1T[:, c, 0:TILE],
                              (nmu_r if for_r else nmu_k)[:, c:c + 1]).then_inc(prev_done, 1)

            def u4_block(u, tb):
                if tb % 2 == 0:
                    act.wait_ge(nm[3], 2 * u + V_ORDER.index(tb) // 2 + 1)
                normalise(sig[:, tb, :], sig[:, tb, :], 3, tb).then_inc(u4_done, 1)

            t_parity = [0]

            def first():
                act.preload_act_table_set("natural_log_exp_and_others")
                act.wait_ge(s_asoft, 1)
                nc.scalar.activation(a_tmp[:, 0:1], a_tmp[:, 0:1], ACT.Exp).then_inc(s_asoft, 1)
                act.wait_ge(s_asoft, 2)
                nc.scalar.activation(a_tmp[:, 0:1], a_tmp[:, 0:1], ACT.Ln, bias=1.0).then_inc(s_asoft, 1)
                act.wait_ge(s_const, CONSTANTS)
                xn_block(0, 0)
                xn_block(0, 1)
                xn_block(0, 2)
                xn_block(0, 3)
                for tb in range(TB):
                    xT_hi_block(0, tb)
                softplus_exp_log(0)
                decay(0)
                t_parity[0] = 1
                for tb in range(TB):
                    xn_block(1, tb)
                for tb in range(3):
                    xT_hi_block(1, tb)
                u2_block(0, 0, 0, 0)
                u2_block(0, 0, 0, 1)
                xT_hi_block(1, 3)
                u2_block(0, 0, 0, 2)
                u2_block(0, 0, 0, 3)
                for tb in range(TB):
                    x1T_block(0, 0, tb)
                act.wait_ge(s_wsplit, 8)
                for c in range(CH):
                    scale_prev(0, 0, c)

            def step(t, par, j, more):
                u = t - 1
                t_parity[0] = 1 - par
                softplus_exp_log(t)
                if not isinstance(t, int) or t >= 2:
                    u4_block(t - 2, 0)
                    u4_block(t - 2, 1)
                k_square(u, 0)
                scale_prev(u, 1, 0)
                scale_prev(u, 1, 1)
                decay(t)
                k_square(u, 1)
                scale_prev(u, 1, 2)
                scale_prev(u, 1, 3)
                k_square(u, 2)
                if more:
                    xn_block(t + 1, 0)
                    xn_block(t + 1, 1)
                k_square(u, 3)
                if more:
                    xn_block(t + 1, 2)
                    xn_block(t + 1, 3)
                if more:
                    for tb in range(3):
                        xT_hi_block(t + 1, tb)
                u2_block(t, par, j, 0)
                u2_block(t, par, j, 1)
                if more:
                    xT_hi_block(t + 1, 3)
                sigmoid(u, 0)
                u2_block(t, par, j, 2)
                u2_block(t, par, j, 3)
                sigmoid(u, 1)
                x1T_block(t, par, 0)
                x1T_block(t, par, 1)
                sigmoid(u, 2)
                sigmoid(u, 3)
                x1T_block(t, par, 2)
                x1T_block(t, par, 3)
                for c in range(CH):
                    scale_prev(t, 0, c)
                u4_block(u, 2)
                u4_block(u, 3)

            def last():
                u = NT - 1
                u4_block(u - 1, 0)
                u4_block(u - 1, 1)
                for f in range(CH):
                    k_square(u, f)
                    scale_prev(u, 1, f)
                for tb in range(TB):
                    sigmoid(u, tb)
                for tb in V_ORDER:
                    u4_block(u, tb)

            run(act, first, step, last)

        @block.vector
        def _(dve):
            v = nc.vector

            def norm_stats(kind, tb, in_ap, bn, done, n):
                v.bn_stats(stats[:, kind, tb % 2, :], in_ap).then_inc(bn, 1)
                dve.drain()
                v.bn_aggr(mv[:, kind, tb, :], stats[:, kind, tb % 2, :]).then_inc(done, 1)

            def ln1_stats(t, par, j):
                dve.wait_ge(s_xl[par], 16 * (j + 1))
                for tb in range(TB):
                    norm_stats(0, tb, x[:, par, tb, :], bn1, mv1, 4 * t + tb)

            def xT_lo_block(t, tb):
                dve.wait_ge(xhi_done, 4 * t + tb + 1)
                ks = slice(tb * P, (tb + 1) * P)
                v.tensor_tensor(xT_lo[:, :, ks], tr_bank[tb % 2][:, :].rearrange("p (c k) -> p c k", c=CH),
                                xT_hi[:, :, ks].bitcast(F32), ALU.subtract).then_inc(xlo_done, 1)

            def softplus_clamp(t):
                dve.wait_ge(z_ready, t + 1)
                v.tensor_scalar(soft[:, :], z_bank[:, :], bdelta_v, SOFTPLUS_MAX, ALU.add, ALU.min).then_inc(zc_done, 1)

            def log_decay(t, par):
                dve.wait_ge(l_done, t + 1)
                v.scalar_tensor_tensor(delta[:, :], z_bank[:, :], bdelta_v, soft[:, :], ALU.add, ALU.max).then_inc(delta_done, 1)
                dve.wait_ge(delta_done, t + 1)
                v.tensor_scalar(soft[:, :], delta[:, :], a_neg[:, 0:1], None, ALU.mult).then_inc(a_done, 1)
                v.tensor_copy(cum[:, 0:1], cum_carry[:, par:par + 1]).then_inc(col0_done, 1)
                dve.wait_ge(a_done, t + 1)
                dve.wait_ge(col0_done, t + 1)
                v.tensor_tensor_scan(cum[:, 1:], soft[:, :], soft[:, :], cum[:, 0:1], ALU.add, ALU.bypass).then_inc(cum_done, 1)
                dve.wait_ge(cum_done, t + 1)
                v.tensor_copy(cum_carry[:, par:par + 1], cum[:, TILE:TILE + 1]).then_inc(cumc_done, 1)
                dve.wait_ge(cumc_done, t + 1)
                v.tensor_scalar(cum[:, :], cum[:, :], -CLIP, CLIP, ALU.max, ALU.min).then_inc(c_done, 1)
                dve.wait_ge(c_done, t + 1)
                v.tensor_tensor(soft[:, :], cum[:, 1:], cum[:, 0:TILE], ALU.subtract).then_inc(dc_done, 1)
                dve.wait_ge(b_ready, t + 1)
                v.scalar_tensor_tensor(bbar[:, :], b_bank[:, :], bb_v, delta[:, :], ALU.add, ALU.mult).then_inc(bbar_done, 1)

            def recurrence(t, par):
                dve.wait_ge(bbar_done, t + 1)
                dve.wait_ge(g_done, t + 1)
                v.tensor_tensor_scan(delta[:, :], bbar[:, :], soft[:, :], h_carry[:, par:par + 1], ALU.add, ALU.mult).then_inc(h_done, 1)
                dve.wait_ge(h_done, t + 1)
                dve.wait_ge(att_ready, 4 * t)
                v.tensor_copy(h_hi[:, :], delta[:, :]).then_inc(hhi_done, 1)
                v.tensor_copy(h_carry[:, par:par + 1], delta[:, TILE - 1:TILE])
                dve.wait_ge(hhi_done, t + 1)
                v.tensor_tensor(h_lo[:, :], delta[:, :], h_hi[:, :].bitcast(F32), ALU.subtract).then_inc(h_split, 1)

            def k_lo(u, f):
                dve.wait_ge(kahi_done, 4 * u + f + 1)
                v.tensor_tensor(relu[:, f % 2, :], relu[:, f % 2, :], relu[:, f % 2, :], ALU.mult).then_inc(sq_done, 1)
                dve.wait_ge(sq_done, 4 * u + f + 1)
                v.tensor_tensor(ka_lo[:, f, :], relu[:, f % 2, :], ka_hi[:, f, :].bitcast(F32), ALU.subtract).then_inc(ka_split, 1)

            def mix(u, for_r, c):
                mu = (mu_r if for_r else mu_k)[:, c:c + 1]
                dve.wait_ge(prev_done, 8 * u + 4 * for_r + c + 1)
                v.scalar_tensor_tensor(mixf[:, c, :], x1T[:, c, 1:], mu, mixf[:, c, :], ALU.mult, ALU.add).then_inc(mixf_done, 1)

            def mix_split_chunk(u, for_r, c):
                n = 8 * u + 4 * for_r + c
                dve.wait_ge(mixf_done, n + 1)
                if c == 0:
                    dve.wait_ge(k_ready if for_r else r_ready, 4 * u + 4 * for_r)
                v.tensor_copy(mix_hi[:, c, :], mixf[:, c, :]).then_inc(mixhi_done, 1)
                dve.wait_ge(mixhi_done, n + 1)
                v.tensor_tensor(mix_lo[:, c, :], mixf[:, c, :], mix_hi[:, c, :].bitcast(F32), ALU.subtract).then_inc(mix_split, 1)

            def ln2_stats(t, tb):
                dve.wait_ge(att_ready, 4 * t + tb + 1)
                norm_stats(1, tb, av_bank[tb][:, :], bn2, mv2, 4 * t + tb)

            def ln3_stats(t, par, tb):
                dve.wait_ge(x1_done, 4 * t + tb + 1)
                norm_stats(2, tb, x1[:, par, tb, :], bn3, mv3, 4 * t + tb)

            def x1n_block(t, par, tb):
                if tb == 0:
                    dve.wait_ge(t2_ready, 4 * t)
                if tb % 2 == 0:
                    dve.wait_ge(rs[2], 2 * t + tb // 2 + 1)
                v.tensor_scalar(x1n[:, tb, :], x1[:, par, tb, :], mv[:, 2, tb, 0:1], rstd[:, 2, tb:tb + 1],
                                ALU.subtract, ALU.mult).then_inc(x1n_done, 1)

            def gate(u, n):
                tb = V_ORDER[n]
                if n == 0:
                    dve.wait_ge(sig_done, 4 * u + 4)
                dve.wait_ge(v_ready, 4 * u + n + 1)
                v.tensor_tensor(sig[:, tb, :], av_bank[tb][:, :], sig[:, tb, :], ALU.mult).then_inc(w_done, 1)
                dve.wait_ge(w_done, 4 * u + n + 1)
                norm_stats(3, tb, sig[:, tb, :], bn4, mv4, 4 * u + n)

            def split(n, hi, lo):
                stage = STAGED[n]
                dve.wait_ge(s_w[n], 16)
                v.tensor_copy(hi, stage).then_inc(s_whi, 1)
                dve.wait_ge(s_whi, SPLITS.index(n) + 1)
                v.tensor_tensor(lo, stage, hi.bitcast(F32), ALU.subtract).then_inc(s_wsplit, 1)

            def first():
                v.memset(cum_carry[:, :], 0.0).then_inc(s_const, 1)
                v.memset(h_carry[:, :], 0.0).then_inc(s_const, 1)
                v.memset(x1T_carry[:, :, :], 0.0).then_inc(s_const, 1)
                v.memset(mhalf[:, :], -0.5).then_inc(s_const, 1)
                v.memset(epsilon[:, :], EPS).then_inc(s_const, 1)
                v.memset(minus1[:, :], -1.0).then_inc(s_const, 1)
                v.memset(bbar[:, 0:P], 1.0).then_inc(s_const, 1)
                dve.wait_ge(s_const, 7)
                v.tensor_copy(ones[:, :], bbar[:, 0:P]).then_inc(s_const, 1)
                dve.wait_ge(s_vec, 16)
                v.tensor_scalar(a_tmp[:, 0:1], A_v, SOFTPLUS_MAX, None, ALU.min).then_inc(s_asoft, 1)
                v.tensor_scalar(nmu, vecs[:, 3:3 + 2 * CH], -1.0, 1.0, ALU.mult, ALU.add).then_inc(s_const, 1)
                dve.wait_ge(s_asoft, 3)
                v.tensor_scalar(a_neg[:, 0:1], a_tmp[:, 0:1], A_v, -1.0, ALU.max, ALU.mult).then_inc(s_const, 1)
                dve.wait_ge(s_const, CONSTANTS)
                ln1_stats(0, 0, 0)
                split(0, wdelta_hi[:, :, :].rearrange("p c n -> p (c n)"), wdelta_lo[:, :, :].rearrange("p c n -> p (c n)"))
                split(1, wb_hi[:, :, :].rearrange("p c n -> p (c n)"), wb_lo[:, :, :].rearrange("p c n -> p (c n)"))
                for tb in range(TB):
                    xT_lo_block(0, tb)
                split(2, wd_hi[:, :, :], wd_lo[:, :, :])
                split(3, wc_hi[:, :], wc_lo[:, :])
                dve.wait_ge(s_w[4], 16)
                dve.wait_ge(s_w[5], 16)
                b_sum = STAGED[4]
                v.tensor_tensor(b_sum, STAGED[4], STAGED[5], ALU.add).then_inc(s_bias, 1)
                dve.wait_ge(s_bias, 1)
                v.tensor_scalar(b_sum, b_sum, 2.0 / P, None, ALU.mult).then_inc(s_bias, 1)
                dve.wait_ge(s_bias, 2)
                v.tensor_copy(bias_rows[:, :], b_sum).then_inc(s_bias, 1)
                dve.wait_ge(s_bias, 3)
                v.tensor_tensor(bias_rows[P // 2:, :], b_sum[P // 2:, :], bias_rows[P // 2:, :].bitcast(F32),
                                ALU.subtract).then_inc(s_wsplit, 1)
                softplus_clamp(0)
                ln1_stats(1, 1, 0)
                log_decay(0, 0)
                recurrence(0, 0)
                ln2_stats(0, 0)
                xT_lo_block(1, 0)
                ln2_stats(0, 1)
                xT_lo_block(1, 1)
                ln2_stats(0, 2)
                xT_lo_block(1, 2)
                ln3_stats(0, 0, 0)
                ln2_stats(0, 3)
                ln3_stats(0, 0, 1)
                xT_lo_block(1, 3)
                x1n_block(0, 0, 0)
                x1n_block(0, 0, 1)
                ln3_stats(0, 0, 2)
                ln3_stats(0, 0, 3)
                x1n_block(0, 0, 2)
                x1n_block(0, 0, 3)
                split(6, wk_hi[:, :, :], wk_lo[:, :, :])
                split(7, wr_hi[:, :, :], wr_lo[:, :, :])
                split(8, wv_hi[:, :, :], wv_lo[:, :, :])
                for c in range(CH):
                    mix(0, 0, c)
                for c in range(CH):
                    mix_split_chunk(0, 0, c)

            def step(t, par, j, more):
                u = t - 1
                softplus_clamp(t)
                if more:
                    ln1_stats(t + 1, 1 - par, j + par)
                log_decay(t, par)
                k_lo(u, 0)
                recurrence(t, par)
                k_lo(u, 1)
                mix(u, 1, 0)
                mix(u, 1, 1)
                k_lo(u, 2)
                mix(u, 1, 2)
                mix(u, 1, 3)
                k_lo(u, 3)
                mix_split_chunk(u, 1, 0)
                ln2_stats(t, 0)
                if more:
                    xT_lo_block(t + 1, 0)
                mix_split_chunk(u, 1, 1)
                ln2_stats(t, 1)
                mix_split_chunk(u, 1, 2)
                if more:
                    xT_lo_block(t + 1, 1)
                mix_split_chunk(u, 1, 3)
                ln2_stats(t, 2)
                if more:
                    xT_lo_block(t + 1, 2)
                ln3_stats(t, par, 0)
                ln2_stats(t, 3)
                ln3_stats(t, par, 1)
                if more:
                    xT_lo_block(t + 1, 3)
                x1n_block(t, par, 0)
                x1n_block(t, par, 1)
                ln3_stats(t, par, 2)
                ln3_stats(t, par, 3)
                x1n_block(t, par, 2)
                x1n_block(t, par, 3)
                for c in range(CH):
                    mix(t, 0, c)
                    mix_split_chunk(t, 0, c)
                    gate(u, c)

            def last():
                u = NT - 1
                for f in range(CH):
                    k_lo(u, f)
                    mix(u, 1, f)
                for c in range(CH):
                    mix_split_chunk(u, 1, c)
                for n in range(TB):
                    gate(u, n)

            run(dve, first, step, last)

        @block.gpsimd
        def _(pool):
            g = nc.gpsimd

            def scales(kind, tb, blocks, ready, n_ready, n):
                s = slice(tb, tb + blocks)
                pool.wait_ge(ready, n_ready)
                g.tensor_tensor(vare[:, kind, s], mv[:, kind, s, 1], epsilon[:, 0:blocks], ALU.add).then_inc(ve[kind], 1)
                pool.wait_ge(ve[kind], n + 1)
                g.tensor_tensor(rstd[:, kind, s], vare[:, kind, s], mhalf[:, 0:blocks], ALU.pow).then_inc(rs[kind], 1)
                if kind == 2:
                    return
                pool.wait_ge(rs[kind], n + 1)
                g.tensor_tensor(nmr[:, kind, s], mv[:, kind, s, 0], rstd[:, kind, s], ALU.mult).then_inc(nmp[kind], 1)
                pool.wait_ge(nmp[kind], n + 1)
                g.tensor_tensor(nmr[:, kind, s], nmr[:, kind, s], minus1[:, 0:blocks], ALU.mult).then_inc(nm[kind], 1)

            def x1_scales(t, pair):
                scales(1, 2 * pair, 2, mv2, 4 * t + 2 * pair + 2, 2 * t + pair)

            def x1_add(t, par, tb):
                pool.wait_ge(u2_done, 4 * t + tb + 1)
                g.tensor_tensor(x1[:, par, tb, :], x1[:, par, tb, :], x[:, par, tb, :], ALU.add).then_inc(x1_done, 1)

            def x1n_scales(t, pair):
                scales(2, 2 * pair, 2, mv3, 4 * t + 2 * pair + 2, 2 * t + pair)

            def y_scales(u, pair):
                scales(3, V_ORDER[2 * pair], 2, mv4, 4 * u + 2 * pair + 2, 2 * u + pair)

            def y_add(u, par, n):
                tb = V_ORDER[n]
                pool.wait_ge(u4_done, 4 * u + n + 1)
                g.tensor_tensor(x1[:, par, tb, :], x1[:, par, tb, :], sig[:, tb, :], ALU.add).then_inc(y_done, 1)

            def x1_tile(t, par):
                x1_scales(t, 0)
                x1_add(t, par, 0)
                x1_add(t, par, 1)
                x1_scales(t, 1)
                x1n_scales(t, 0)
                x1_add(t, par, 2)
                x1_add(t, par, 3)
                x1n_scales(t, 1)

            def y_tile(u, par):
                for pair in range(2):
                    y_scales(u, pair)
                    y_add(u, par, 2 * pair)
                    y_add(u, par, 2 * pair + 1)

            def first():
                g.memset(ident[:, :], 0.0).then_inc(s_ident, 1)
                pool.wait_ge(s_ident, 1)
                g.affine_select(out=ident[:, :], in_=ident[:, :], compare_op=ALU.not_equal, fill=1.0, base=0,
                                pattern=[[-1, P]], channel_multiplier=1).then_inc(s_ident, 1)
                pool.wait_ge(s_const, CONSTANTS)
                scales(0, 0, TB, mv1, 4, 0)
                scales(0, 0, TB, mv1, 8, 1)
                x1_tile(0, 0)

            def step(t, par, j, more):
                if more:
                    scales(0, 0, TB, mv1, 4 * t + 8, t + 1)
                x1_tile(t, par)
                y_tile(t - 1, 1 - par)

            def last():
                y_tile(NT - 1, 1)

            run(pool, first, step, last)


def kernel(**inputs):
    import numpy as _np
    import concourse.bacc as _bacc
    from concourse import mybir as _mybir
    from concourse.bass_utils import run_bass_kernel_spmd as _run

    a = {n.split("_", 2)[2]: _np.asarray(v) for n, v in inputs.items()}
    n_chunks = a["mu_r"].shape[0] // 128

    def chunked(w):
        return w.reshape(w.shape[0] // 128, 128, w.shape[1]).transpose(1, 0, 2)

    def rows(b):
        return _np.broadcast_to(b[None, :], (128, b.shape[0]))

    vectors = _np.concatenate([a["A"][:, None], a["bb"][:, None], a["bdelta"][:, None],
                               a["mu_r"].reshape(n_chunks, 128).T, a["mu_k"].reshape(n_chunks, 128).T], axis=1)
    arrays = {
        "x": a["x"], "vectors": vectors, "bc": rows(a["bc"]), "bd": rows(a["bd"]),
        "w_delta": chunked(a["Wdelta"]).reshape(128, -1), "w_b": chunked(a["Wb"]).reshape(128, -1),
        "w_c": a["Wc"], "w_d": chunked(a["Wd"]),
        "w_r": chunked(a["W_r"].T), "w_k": chunked(a["W_k"].T), "w_v": chunked(a["W_v"].T),
    }
    arrays = {k: _np.ascontiguousarray(v) for k, v in arrays.items()}
    nc = _bacc.Bacc("TRN2", target_bir_lowering=False, num_devices=1, dynamic_dma_scratch_size=1024)
    args = {k: nc.dram_tensor(f"in_{k}_dram", v.shape, _mybir.dt.from_np(v.dtype), kind="ExternalInput").ap()
            for k, v in arrays.items()}
    out = nc.dram_tensor("out_dram", a["x"].shape, _mybir.dt.float32, kind="ExternalOutput").ap()
    state_space_mixer_and_channel_mixer(nc, args["x"], args["vectors"], args["bc"], args["bd"], args["w_delta"], args["w_b"],
                                        args["w_c"], args["w_d"], args["w_r"], args["w_k"], args["w_v"], out)
    r = _run(nc, [{f"in_{k}_dram": v for k, v in arrays.items()}], core_ids=[0])
    return r.results[0]["out_dram"]
```

```python
from contextlib import ExitStack

import concourse.bass as bass
from concourse import mybir

ALU = mybir.AluOpType
ACT = mybir.ActivationFunctionType
F32 = mybir.dt.float32
F32R = mybir.dt.float32r

P = 128
TILE = 512
TB = TILE // P
EPS = 1e-5
CLIP = 20.0
SOFTPLUS_MAX = 30.0


def state_space_mixer_and_channel_mixer(nc, x_in, vectors, bc, bd, w_delta, w_b, w_c, w_d, w_r, w_k, w_v, out):
    NB, T, DM = x_in.shape
    DH = w_c.shape[0]
    CH = DM // P
    NT = NB * T // TILE
    assert NB == 2 and DH == P and DM == 512 and NT % 2 == 0

    x_d = x_in.rearrange("b (n p) d -> p (b n) d", p=P)
    out_d = out.rearrange("b (n p) d -> p (b n) d", p=P)

    with ExitStack() as ctx:
        def sb(name, shape, dt=F32):
            return ctx.enter_context(nc.sbuf_tensor(name, shape, dt))

        def bank(name):
            return ctx.enter_context(nc.psum_tensor(name, [P, 512], F32))

        def sem(name):
            return ctx.enter_context(nc.semaphore(name))

        wdelta_hi, wdelta_lo = sb("wdelta_hi", [P, CH, DH], F32R), sb("wdelta_lo", [P, CH, DH], F32R)
        wb_hi, wb_lo = sb("wb_hi", [P, CH, DH], F32R), sb("wb_lo", [P, CH, DH], F32R)
        wc_hi, wc_lo = sb("wc_hi", [P, DM], F32R), sb("wc_lo", [P, DM], F32R)
        wd_hi, wd_lo = sb("wd_hi", [P, CH, DM], F32R), sb("wd_lo", [P, CH, DM], F32R)
        wr_hi, wr_lo = sb("wr_hi", [P, CH, DM], F32R), sb("wr_lo", [P, CH, DM], F32R)
        wk_hi, wk_lo = sb("wk_hi", [P, CH, DM], F32R), sb("wk_lo", [P, CH, DM], F32R)
        wv_hi, wv_lo = sb("wv_hi", [P, CH, DM], F32R), sb("wv_lo", [P, CH, DM], F32R)
        bias = sb("bias", [P, DM])
        ident = sb("ident", [P, P])
        vecs = sb("vecs", [P, vectors.shape[1]])
        x = sb("x", [P, 2, TB, DM])
        x1 = sb("x1", [P, 2, TB, DM])
        xn = sb("xn", [P, TB, DM])
        xT_hi, xT_lo = sb("xT_hi", [P, CH, TILE], F32R), sb("xT_lo", [P, CH, TILE], F32R)
        x1n = sb("x1n", [P, TB, DM])
        x1T = sb("x1T", [P, CH, TILE + 1])
        mix_hi, mix_lo = sb("mix_hi", [P, CH, TILE], F32R), sb("mix_lo", [P, CH, TILE], F32R)
        ka_hi, ka_lo = sb("ka_hi", [P, CH, TILE], F32R), sb("ka_lo", [P, CH, TILE], F32R)
        sig = sb("sig", [P, TB, DM])
        relu = sb("relu", [P, 2, TILE])
        mixf = sb("mixf", [P, CH, TILE])
        soft = sb("soft", [P, TILE])
        delta = sb("delta", [P, TILE])
        bbar = sb("bbar", [P, TILE])
        cum = sb("cum", [P, TILE + 1])
        h_hi, h_lo = sb("h_hi", [P, TILE], F32R), sb("h_lo", [P, TILE], F32R)
        smalls = sb("smalls", [P, 4 * 2 * 6 + 4 * TB * 5 + 3 * TB + 2 * CH + 2 + 2 * NB + NB * CH])
        taken = [0]

        def small(*shape):
            n = 1
            for k in shape:
                n *= k
            part = smalls[:, taken[0]:taken[0] + n]
            taken[0] += n
            names = " ".join("abc"[:len(shape)])
            return part.rearrange(f"p ({names}) -> p {names}", **dict(zip("abc", shape))) if len(shape) > 1 else part

        stats = small(4, 2, 6)
        mv = small(4, TB, 2)
        vare, rstd, nmr = small(4, TB), small(4, TB), small(4, TB)
        mhalf, epsilon, minus1 = small(TB), small(TB), small(TB)
        nmu = small(2 * CH)
        a_neg, a_tmp = small(1), small(1)
        cum_carry, h_carry = small(NB), small(NB)
        x1T_carry = small(NB, CH)

        A_v, bb_v, bdelta_v = vecs[:, 0:1], vecs[:, 1:2], vecs[:, 2:3]
        mu_r, mu_k = vecs[:, 3:3 + CH], vecs[:, 3 + CH:3 + 2 * CH]
        nmu_r, nmu_k = nmu[:, 0:CH], nmu[:, CH:2 * CH]

        kr_bank = [bank("kr0"), bank("kr1")]
        z_bank, b_bank = bank("zb"), bank("bb")
        av_bank = [bank("av0"), bank("av1"), z_bank, b_bank]
        tr_bank = [bank("tr0"), bank("tr1")]

        def att_bank(t, tb):
            return kr_bank[tb - 2] if isinstance(t, int) and t == 0 and tb >= 2 else av_bank[tb]

        def t1_bank(t, tb):
            return kr_bank[tb - 2] if isinstance(t, int) and t == 0 and tb >= 2 else tr_bank[tb % 2]

        s_vec, s_w = sem("vectors_loaded"), [sem(f"weight{i}_loaded") for i in range(9)]
        s_stored = [sem("stored_even"), sem("stored_odd")]
        s_ident, s_const, s_asoft = sem("ident_ready"), sem("constants_ready"), sem("a_softplus")
        s_wsplit, s_whi, s_bias = sem("weights_split"), sem("weight_hi"), sem("bias_ready")
        s_krv_hi, s_kr_split = sem("krv_weight_hi"), sem("kr_weights_split")
        nmp = [sem(f"ln{i + 1}_mean_rstd") for i in range(4)]
        s_x0 = [sem(f"x_tile0_block{tb}_loaded") for tb in range(TB)]
        s_xl = [sem("x_loaded_even"), sem("x_loaded_odd")]
        z_ready, b_ready = sem("z_ready"), sem("b_ready")
        summed = sem("bias_added")
        k_ready, att_ready, t1_ready = sem("k_ready"), sem("att_ready"), sem("t1_ready")
        r_ready, t2_ready, v_ready = sem("r_ready"), sem("t2_ready"), sem("v_ready")
        zc_done, e_done, l_done = sem("z_clamped"), sem("exp_done"), sem("log_done")
        delta_done, a_done, cum_done, cumc_done = sem("delta_done"), sem("a_done"), sem("cum_done"), sem("cum_carried")
        c_done, dc_done, g_done, bbar_done = sem("clip_done"), sem("step_done"), sem("decay_done"), sem("bbar_done")
        col0_done, h_done, hhi_done, h_split = sem("cum_col0"), sem("h_done"), sem("h_hi_done"), sem("h_split")
        relu_done, kahi_done, sq_done, ka_split = sem("relu_done"), sem("ka_hi_done"), sem("square_done"), sem("ka_split")
        bn1, mv1, bn2, mv2 = sem("bn1"), sem("mv1"), sem("bn2"), sem("mv2")
        bn3, mv3, bn4, mv4 = sem("bn3"), sem("mv3"), sem("bn4"), sem("mv4")
        rs = [sem(f"ln{i + 1}_rstd") for i in range(4)]
        ve = [sem(f"ln{i + 1}_vare") for i in range(4)]
        nm = [sem(f"ln{i + 1}_scales") for i in range(4)]
        xn_done, xhi_done, xlo_done = sem("xn_done"), sem("xT_hi_done"), sem("xT_lo_done")
        u2_done, x1_done, x1n_done, evac_done = sem("u2_done"), sem("x1_done"), sem("x1n_done"), sem("x1T_done")
        x1c_done = sem("x1T_col0")
        prev_done, mixf_done, mixhi_done, mix_split = sem("prev_scaled"), sem("mixf_done"), sem("mix_hi_done"), sem("mix_split")
        sig_done, w_done, u4_done, y_done = sem("sig_done"), sem("w_done"), sem("u4_done"), sem("y_done")

        block = ctx.enter_context(nc.Block())

        def run(eng, first, step, last):
            first()
            step(1, 1, 0, True)
            with eng.Fori(1, NT // 2 - 1) as i:
                step(2 * i, 0, i, True)
                step(2 * i + 1, 1, i, True)
            step(NT - 2, 0, NT // 2 - 1, eng is not nc.sync)
            step(NT - 1, 1, NT // 2 - 1, False)
            last()

        WEIGHTS = [(w_delta, x1n[:, 0, :]), (w_b, x1n[:, 1, :]), (w_d, x1[:, 0, :, :]), (w_c, x1n[:, 2, :]),
                   (bc, x1n[:, 3, :]), (bd, relu[:, 0, :]), (w_k, x1[:, 1, :, :]), (w_r, sig[:, :, :]), (w_v, mixf[:, :, :])]
        STAGED = [s for _, s in WEIGHTS]
        SPLITS = [0, 1, 2, 3]
        KRV = [(wk_hi, wk_lo), (wr_hi, wr_lo), (wv_hi, wv_lo)]
        CONSTANTS = 8
        V_ORDER = [2, 3, 0, 1]

        def gated(u, tb):
            return (xn if isinstance(u, int) and u == NT - 1 else sig)[:, tb, :]

        @block.sync
        def _(sp):
            def load_x(par, block):
                sp.dma_start(x[:, par, :, :], x_d[:, bass.ds(block + par * T // P, TB), :]).then_inc(s_xl[par], 16)

            def load_weight(n):
                src, dst = WEIGHTS[n]
                sp.dma_start(dst, src).then_inc(s_w[n], 16)

            for tb in range(TB):
                sp.dma_start(x[:, 0, tb, :], x_d[:, tb, :]).then_inc(s_x0[tb], 16)
            sp.dma_start(vecs[:, :], vectors).then_inc(s_vec, 16)
            for n in range(6):
                load_weight(n)
            load_x(1, 0)
            for n in range(6, 9):
                load_weight(n)

            def step(t, par, j, more):
                if more:
                    sp.wait_ge(x1_done, 4 * t + 4)
                    load_x(par, (j + 1) * TB)
                sp.wait_ge(y_done, 4 * t)
                sp.dma_start(out_d[:, bass.ds((j + par - 1) * TB + (1 - par) * T // P, TB), :],
                             x1[:, 1 - par, :, :]).then_inc(s_stored[1 - par], 16)

            def first():
                sp.wait_ge(x1_done, 4)
                load_x(0, TB)

            run(sp, first, step, lambda: None)
            for n, tb in enumerate(V_ORDER):
                sp.wait_ge(y_done, 4 * NT - 3 + n)
                sp.dma_start(out_d[:, NT * TB - TB + tb, :], x1[:, 1, tb, :]).then_inc(s_stored[1], 16)
            sp.wait_ge(s_stored[0], 16 * NT // 2)
            sp.wait_ge(s_stored[1], 16 * (NT // 2 - 1 + TB))

        @block.tensor
        def _(pe):
            def three(dst, pairs, first=True, last=True):
                for n, (a_hi, a_lo, b_hi, b_lo) in enumerate(pairs):
                    pe.matmul(dst, a_hi, b_hi, start=first and n == 0, stop=False)
                    pe.matmul(dst, a_hi, b_lo, start=False, stop=False)
                    mm = pe.matmul(dst, a_lo, b_hi, start=False, stop=last and n == len(pairs) - 1)
                return mm

            def cols(w, c, m):
                return w[:, c, m * P:(m + 1) * P]

            def proj(t, z_free, b_free):
                pe.wait_ge(xlo_done, 4 * t + 4)
                if z_free is not None:
                    pe.wait_ge(*z_free)
                three(z_bank[:, :], [(wdelta_hi[:, c, :], wdelta_lo[:, c, :], xT_hi[:, c, :], xT_lo[:, c, :])
                                     for c in range(CH)]).then_inc(z_ready, 1)
                if b_free is not None:
                    pe.wait_ge(*b_free)
                three(b_bank[:, :], [(wb_hi[:, c, :], wb_lo[:, c, :], xT_hi[:, c, :], xT_lo[:, c, :])
                                     for c in range(CH)]).then_inc(b_ready, 1)

            def att_x(t, tb):
                if tb == 0 and (not isinstance(t, int) or t >= 2):
                    pe.wait_ge(w_done, 4 * t - 4)
                three(att_bank(t, tb)[:, :], [(cols(xT_hi, c, tb), cols(xT_lo, c, tb), wd_hi[:, c, :], wd_lo[:, c, :])
                                              for c in range(CH)], last=False)

            def att_h(t, tb):
                if tb == 0:
                    pe.wait_ge(h_split, t + 1)
                hs = slice(tb * P, (tb + 1) * P)
                three(att_bank(t, tb)[:, :], [(h_hi[:, hs], h_lo[:, hs], wc_hi[:, :], wc_lo[:, :])],
                      first=False).then_inc(att_ready, 1)

            def att(t, t1_next):
                for tb in range(TB):
                    att_x(t, tb)
                    att_h(t, tb)
                    if t1_next:
                        t1(t + 1, tb)

            def t1(t, tb, after_t2=True):
                pe.wait_ge(xn_done, 4 * t + tb + 1)
                if tb >= 2 and t1_bank(t, tb) is tr_bank[tb % 2]:
                    pe.wait_ge(xlo_done, 4 * t + tb - 1)
                elif after_t2:
                    pe.wait_ge(evac_done, 4 * (t - 2) + 3 + tb)
                for c in range(CH):
                    mm = pe.transpose(t1_bank(t, tb)[:, c * P:(c + 1) * P], xn[:, tb, c * P:(c + 1) * P], ident[:, :])
                mm.then_inc(t1_ready, 1)

            def t2(t, tb, after_t1):
                pe.wait_ge(x1n_done, 4 * t + tb + 1)
                if tb >= 2:
                    pe.wait_ge(evac_done, 4 * t + tb - 1)
                elif after_t1:
                    pe.wait_ge(xlo_done, 4 * t + 7 + tb)
                else:
                    pe.wait_ge(evac_done, 4 * t - 1 + tb)
                for c in range(CH):
                    mm = pe.transpose(tr_bank[tb % 2][:, c * P:(c + 1) * P], x1n[:, tb, c * P:(c + 1) * P], ident[:, :])
                mm.then_inc(t2_ready, 1)

            def k_product(u):
                pe.wait_ge(mix_split, 8 * u + 4)
                pe.wait_ge(sig_done, 4 * u)
                for f in range(CH):
                    if f >= 2:
                        pe.wait_ge(relu_done, 4 * u + f - 1)
                    three(kr_bank[f % 2][:, :], [(cols(wk_hi, c, f), cols(wk_lo, c, f), mix_hi[:, c, :], mix_lo[:, c, :])
                                                 for c in range(CH)]).then_inc(k_ready, 1)

            def r_product(u, tb, m_hi=mix_hi, m_lo=mix_lo):
                if tb == 0:
                    pe.wait_ge(mix_split, 8 * u + 8)
                if tb < 2:
                    pe.wait_ge(relu_done, 4 * u + 3 + tb)
                else:
                    pe.wait_ge(sig_done, 4 * u + tb - 1)
                three(kr_bank[tb % 2][:, :], [(cols(m_hi, c, tb), cols(m_lo, c, tb), wr_hi[:, c, :], wr_lo[:, c, :])
                                              for c in range(CH)]).then_inc(r_ready, 1)

            def v_product(u, tb, after_att=True):
                if tb == V_ORDER[0]:
                    pe.wait_ge(ka_split, 4 * u + 4)
                    if after_att:
                        pe.wait_ge(summed, 4 * u + 8)
                if not after_att:
                    pe.wait_ge(w_done, 4 * u - 3 + V_ORDER.index(tb))
                three(av_bank[tb][:, :], [(cols(ka_hi, f, tb), cols(ka_lo, f, tb), wv_hi[:, f, :], wv_lo[:, f, :])
                                              for f in range(CH)]).then_inc(v_ready, 1)

            def first():
                pe.wait_ge(s_ident, 2)
                for tb in range(TB):
                    t1(0, tb, after_t2=False)
                pe.wait_ge(s_wsplit, 2)
                proj(0, None, None)
                pe.wait_ge(s_wsplit, 3)
                att_x(0, 0)
                att_x(0, 1)
                pe.wait_ge(s_wsplit, 4)
                att_h(0, 0)
                att_h(0, 1)
                att_x(0, 2)
                att_h(0, 2)
                t1(1, 0, after_t2=False)
                t1(1, 1, after_t2=False)
                att_x(0, 3)
                att_h(0, 3)
                t1(1, 2)
                t1(1, 3)
                proj(1, (delta_done, 1), (bbar_done, 1))
                t2(0, 0, after_t1=True)
                t2(0, 1, after_t1=True)
                pe.wait_ge(summed, 4)
                att_x(1, 0)
                t2(0, 2, after_t1=True)
                t2(0, 3, after_t1=True)
                att_x(1, 1)

            def step(t, par, j, more):
                u = t - 1
                if isinstance(t, int) and t == 1:
                    pe.wait_ge(s_kr_split, 1)
                    k_product(u)
                    att_h(t, 0)
                    att_h(t, 1)
                    att_x(t, 2)
                    att_h(t, 2)
                    t1(t + 1, 0)
                    t1(t + 1, 1)
                    att_x(t, 3)
                    att_h(t, 3)
                    t1(t + 1, 2)
                    t1(t + 1, 3)
                    pe.wait_ge(s_kr_split, 2)
                    pe.wait_ge(s_wsplit, 5)
                else:
                    proj(t, (w_done, 4 * t - 7), (w_done, 4 * t - 6))
                    k_product(u)
                    att(t, t1_next=more)
                r_product(u, 0)
                r_product(u, 1)
                r_product(u, 2)
                t2(t, 0, more)
                t2(t, 1, more)
                r_product(u, 3)
                t2(t, 2, more)
                t2(t, 3, more)
                for tb in V_ORDER:
                    v_product(u, tb)

            def last():
                u = NT - 1
                k_product(u)
                for tb in range(TB):
                    r_product(u, tb, xT_hi, xT_lo)
                for tb in V_ORDER:
                    v_product(u, tb, after_att=False)

            run(pe, first, step, last)

        @block.scalar
        def _(act):
            def softplus_exp_log(t):
                act.preload_act_table_set("natural_log_exp_and_others")
                act.wait_ge(zc_done, t + 1)
                nc.scalar.activation(soft[:, :], soft[:, :], ACT.Exp).then_inc(e_done, 1)
                act.wait_ge(e_done, t + 1)
                nc.scalar.activation(soft[:, :], soft[:, :], ACT.Ln, bias=1.0).then_inc(l_done, 1)

            def decay(t):
                act.wait_ge(dc_done, t + 1)
                nc.scalar.activation(soft[:, :], soft[:, :], ACT.Exp).then_inc(g_done, 1)

            def k_square(u, f):
                if f == 0:
                    act.wait_ge(ka_split, 4 * u)
                if f >= 2:
                    act.wait_ge(ka_split, 4 * u + f - 1)
                act.wait_ge(k_ready, 4 * u + f + 1)
                nc.scalar.activation(relu[:, f % 2, :], kr_bank[f % 2][:, :], ACT.Relu).then_inc(relu_done, 1)
                act.wait_ge(relu_done, 4 * u + f + 1)
                nc.scalar.activation(ka_hi[:, f, :], relu[:, f % 2, :], ACT.Square).then_inc(kahi_done, 1)

            def normalise(out_ap, in_ap, kind, tb):
                return nc.scalar.activation(out_ap, in_ap, ACT.Identity, bias=nmr[:, kind, tb:tb + 1],
                                            scale=rstd[:, kind, tb:tb + 1])

            def xn_block(t, tb):
                if isinstance(t, int) and t < 2:
                    if tb % 2 == 0:
                        act.wait_ge(nm[0], 2 * t + tb // 2 + 1)
                elif tb == 0:
                    act.wait_ge(nm[0], t + 3)
                normalise(xn[:, tb, :], x[:, t_parity[0], tb, :], 0, tb).then_inc(xn_done, 1)

            def xT_hi_block(t, tb):
                act.wait_ge(t1_ready, 4 * t + tb + 1)
                nc.scalar.copy(xT_hi[:, :, tb * P:(tb + 1) * P],
                               t1_bank(t, tb)[:, :].rearrange("p (c k) -> p c k", c=CH)).then_inc(xhi_done, 1)

            def u2_block(t, par, tb):
                if tb % 2 == 0:
                    act.wait_ge(nm[1], 2 * t + tb // 2 + 1)
                normalise(x1[:, par, tb, :], x1[:, par, tb, :], 1, tb).then_inc(u2_done, 1)

            def sigmoid(u, tb):
                if tb == 0 and not (isinstance(u, int) and u == NT - 1):
                    act.wait_ge(y_done, 4 * u)
                act.wait_ge(r_ready, 4 * u + tb + 1)
                nc.scalar.activation(gated(u, tb), kr_bank[tb % 2][:, :], ACT.Sigmoid).then_inc(sig_done, 1)

            def x1T_block(t, par, tb):
                psum = tr_bank[tb % 2][:, :].rearrange("p (c k) -> p c k", c=CH)
                if tb == 0:
                    act.wait_ge(mixf_done, 8 * t)
                    nc.scalar.copy(x1T[:, :, 0], x1T_carry[:, par, :]).then_inc(x1c_done, 1)
                act.wait_ge(t2_ready, 4 * t + tb + 1)
                if tb == TB - 1:
                    nc.scalar.copy(x1T_carry[:, par, :], psum[:, :, P - 1]).then_inc(x1c_done, 1)
                nc.scalar.copy(x1T[:, :, 1 + tb * P:1 + (tb + 1) * P], psum).then_inc(evac_done, 1)

            def scale_prev(u, for_r, c):
                if not for_r and c == 0:
                    act.wait_ge(evac_done, 4 * u + 4)
                    act.wait_ge(mix_split, 8 * u)
                elif for_r:
                    act.wait_ge(mix_split, 8 * u + c + 1)
                nc.scalar.mul(mixf[:, c, :], x1T[:, c, 0:TILE],
                              (nmu_r if for_r else nmu_k)[:, c:c + 1]).then_inc(prev_done, 1)

            def mix_round(u, for_r, c):
                n = 8 * u + 4 * for_r + c
                act.wait_ge(mixf_done, n + 1)
                nc.scalar.copy(mix_hi[:, c, :], mixf[:, c, :]).then_inc(mixhi_done, 1)

            def u4_block(u, tb):
                if isinstance(u, int) and u == NT - 1:
                    act.wait_ge(nm[3], 2 * u + V_ORDER.index(tb) + 1)
                elif tb % 2 == 0:
                    act.wait_ge(nm[3], 2 * u + V_ORDER.index(tb) // 2 + 1)
                normalise(gated(u, tb), gated(u, tb), 3, tb).then_inc(u4_done, 1)

            def weight_hi(n):
                act.wait_ge(s_w[6 + n], 16)
                nc.scalar.copy(KRV[n][0][:, :, :], STAGED[6 + n]).then_inc(s_krv_hi, 1)

            t_parity = [0]

            def first():
                act.preload_act_table_set("natural_log_exp_and_others")
                for tb in range(TB):
                    xn_block(0, tb)
                for tb in range(TB):
                    xT_hi_block(0, tb)
                act.wait_ge(s_asoft, 1)
                nc.scalar.activation(a_tmp[:, 0:1], a_tmp[:, 0:1], ACT.Exp).then_inc(s_asoft, 1)
                act.wait_ge(s_asoft, 2)
                nc.scalar.activation(a_tmp[:, 0:1], a_tmp[:, 0:1], ACT.Ln, bias=1.0).then_inc(s_asoft, 1)
                softplus_exp_log(0)
                weight_hi(0)
                decay(0)
                weight_hi(1)
                weight_hi(2)
                t_parity[0] = 1
                for tb in range(TB):
                    xn_block(1, tb)
                xT_hi_block(1, 0)
                xT_hi_block(1, 1)
                u2_block(0, 0, 0)
                u2_block(0, 0, 1)
                xT_hi_block(1, 2)
                xT_hi_block(1, 3)
                u2_block(0, 0, 2)
                u2_block(0, 0, 3)
                softplus_exp_log(1)
                for tb in range(TB):
                    x1T_block(0, 0, tb)
                act.wait_ge(s_wsplit, 5)
                act.wait_ge(s_const, CONSTANTS)
                for c in range(CH):
                    scale_prev(0, 0, c)
                for c in range(CH):
                    mix_round(0, 0, c)
                decay(1)

            def step(t, par, j, more):
                u = t - 1
                t_parity[0] = 1 - par
                if not isinstance(t, int) or t > 1:
                    softplus_exp_log(t)
                if not isinstance(t, int) or t >= 2:
                    u4_block(t - 2, 0)
                    u4_block(t - 2, 1)
                k_square(u, 0)
                scale_prev(u, 1, 0)
                scale_prev(u, 1, 1)
                k_square(u, 1)
                if not isinstance(t, int) or t > 1:
                    decay(t)
                scale_prev(u, 1, 2)
                scale_prev(u, 1, 3)
                k_square(u, 2)
                if more:
                    xn_block(t + 1, 0)
                    xn_block(t + 1, 1)
                k_square(u, 3)
                mix_round(u, 1, 0)
                mix_round(u, 1, 1)
                if more:
                    xT_hi_block(t + 1, 0)
                mix_round(u, 1, 2)
                mix_round(u, 1, 3)
                if more:
                    xn_block(t + 1, 2)
                    xT_hi_block(t + 1, 1)
                    xn_block(t + 1, 3)
                    xT_hi_block(t + 1, 2)
                u2_block(t, par, 0)
                u2_block(t, par, 1)
                if more:
                    xT_hi_block(t + 1, 3)
                sigmoid(u, 0)
                u2_block(t, par, 2)
                u2_block(t, par, 3)
                sigmoid(u, 1)
                sigmoid(u, 2)
                x1T_block(t, par, 0)
                x1T_block(t, par, 1)
                sigmoid(u, 3)
                x1T_block(t, par, 2)
                x1T_block(t, par, 3)
                for c in range(CH):
                    scale_prev(t, 0, c)
                for c in range(CH):
                    mix_round(t, 0, c)
                if more:
                    u4_block(u, 2)
                    u4_block(u, 3)

            def last():
                u = NT - 1
                scale_prev(u, 1, 0)
                scale_prev(u, 1, 1)
                k_square(u, 0)
                scale_prev(u, 1, 2)
                scale_prev(u, 1, 3)
                for f in range(1, CH):
                    k_square(u, f)
                for tb in range(TB):
                    sigmoid(u, tb)
                for tb in V_ORDER:
                    u4_block(u - 1, tb)
                for tb in V_ORDER:
                    u4_block(u, tb)

            run(act, first, step, last)

        @block.vector
        def _(dve):
            v = nc.vector

            def norm_stats(kind, tb, in_ap, bn, done, n):
                v.bn_stats(stats[:, kind, tb % 2, :], in_ap).then_inc(bn, 1)
                dve.drain()
                v.bn_aggr(mv[:, kind, tb, :], stats[:, kind, tb % 2, :]).then_inc(done, 1)

            def ln1_block(t, par, tb):
                norm_stats(0, tb, x[:, par, tb, :], bn1, mv1, 4 * t + tb)

            def ln1_stats(t, par, j):
                dve.wait_ge(s_xl[par], 16 * (j + par))
                for tb in range(TB):
                    ln1_block(t, par, tb)

            def xT_lo_block(t, tb):
                dve.wait_ge(xhi_done, 4 * t + tb + 1)
                ks = slice(tb * P, (tb + 1) * P)
                v.tensor_tensor(xT_lo[:, :, ks], t1_bank(t, tb)[:, :].rearrange("p (c k) -> p c k", c=CH),
                                xT_hi[:, :, ks].bitcast(F32), ALU.subtract).then_inc(xlo_done, 1)

            def softplus_clamp(t):
                dve.wait_ge(z_ready, t + 1)
                v.tensor_scalar(soft[:, :], z_bank[:, :], bdelta_v, SOFTPLUS_MAX, ALU.add, ALU.min).then_inc(zc_done, 1)

            def log_decay(t, par):
                dve.wait_ge(l_done, t + 1)
                v.scalar_tensor_tensor(delta[:, :], z_bank[:, :], bdelta_v, soft[:, :], ALU.add, ALU.max).then_inc(delta_done, 1)
                dve.wait_ge(delta_done, t + 1)
                v.tensor_scalar(soft[:, :], delta[:, :], a_neg[:, 0:1], None, ALU.mult).then_inc(a_done, 1)
                v.tensor_copy(cum[:, 0:1], cum_carry[:, par:par + 1]).then_inc(col0_done, 1)
                dve.wait_ge(a_done, t + 1)
                dve.wait_ge(col0_done, t + 1)
                v.tensor_tensor_scan(cum[:, 1:], soft[:, :], soft[:, :], cum[:, 0:1], ALU.add, ALU.bypass).then_inc(cum_done, 1)
                dve.wait_ge(cum_done, t + 1)
                v.tensor_copy(cum_carry[:, par:par + 1], cum[:, TILE:TILE + 1]).then_inc(cumc_done, 1)
                dve.wait_ge(cumc_done, t + 1)
                v.tensor_scalar(cum[:, :], cum[:, :], -CLIP, CLIP, ALU.max, ALU.min).then_inc(c_done, 1)
                dve.wait_ge(c_done, t + 1)
                v.tensor_tensor(soft[:, :], cum[:, 1:], cum[:, 0:TILE], ALU.subtract).then_inc(dc_done, 1)
                dve.wait_ge(b_ready, t + 1)
                v.scalar_tensor_tensor(bbar[:, :], b_bank[:, :], bb_v, delta[:, :], ALU.add, ALU.mult).then_inc(bbar_done, 1)

            def recurrence(t, par):
                dve.wait_ge(bbar_done, t + 1)
                dve.wait_ge(g_done, t + 1)
                v.tensor_tensor_scan(delta[:, :], bbar[:, :], soft[:, :], h_carry[:, par:par + 1], ALU.add, ALU.mult).then_inc(h_done, 1)
                dve.wait_ge(h_done, t + 1)
                dve.wait_ge(att_ready, 4 * t)
                v.tensor_copy(h_hi[:, :], delta[:, :]).then_inc(hhi_done, 1)
                v.tensor_copy(h_carry[:, par:par + 1], delta[:, TILE - 1:TILE])
                dve.wait_ge(hhi_done, t + 1)
                v.tensor_tensor(h_lo[:, :], delta[:, :], h_hi[:, :].bitcast(F32), ALU.subtract).then_inc(h_split, 1)

            def k_lo(u, f):
                dve.wait_ge(kahi_done, 4 * u + f + 1)
                v.tensor_tensor(relu[:, f % 2, :], relu[:, f % 2, :], relu[:, f % 2, :], ALU.mult).then_inc(sq_done, 1)
                dve.wait_ge(sq_done, 4 * u + f + 1)
                v.tensor_tensor(ka_lo[:, f, :], relu[:, f % 2, :], ka_hi[:, f, :].bitcast(F32), ALU.subtract).then_inc(ka_split, 1)

            def mix(u, for_r, c):
                mu = (mu_r if for_r else mu_k)[:, c:c + 1]
                dve.wait_ge(prev_done, 8 * u + 4 * for_r + c + 1)
                v.scalar_tensor_tensor(mixf[:, c, :], x1T[:, c, 1:], mu, mixf[:, c, :], ALU.mult, ALU.add).then_inc(mixf_done, 1)

            def mix_rest(u, for_r, c, hi=mix_hi, lo=mix_lo):
                dve.wait_ge(mixhi_done, 8 * u + 4 * for_r + c + 1)
                v.tensor_tensor(lo[:, c, :], mixf[:, c, :], hi[:, c, :].bitcast(F32), ALU.subtract).then_inc(mix_split, 1)

            def ln2_stats(t, par, j, tb):
                if tb == 0:
                    dve.wait_ge(s_stored[par], 16 * j)
                dve.wait_ge(att_ready, 4 * t + tb + 1)
                v.tensor_tensor(x1[:, par, tb, :], att_bank(t, tb)[:, :], bias[:, :], ALU.add).then_inc(summed, 1)
                dve.wait_ge(summed, 4 * t + tb + 1)
                norm_stats(1, tb, x1[:, par, tb, :], bn2, mv2, 4 * t + tb)

            def ln3_stats(t, par, tb):
                dve.wait_ge(x1_done, 4 * t + tb + 1)
                norm_stats(2, tb, x1[:, par, tb, :], bn3, mv3, 4 * t + tb)

            def x1n_block(t, par, tb):
                if tb == 0:
                    dve.wait_ge(t2_ready, 4 * t)
                if tb % 2 == 0:
                    dve.wait_ge(rs[2], 2 * t + tb // 2 + 1)
                v.tensor_scalar(x1n[:, tb, :], x1[:, par, tb, :], mv[:, 2, tb, 0:1], rstd[:, 2, tb:tb + 1],
                                ALU.subtract, ALU.mult).then_inc(x1n_done, 1)

            def gate(u, n):
                tb = V_ORDER[n]
                if n == 0:
                    dve.wait_ge(sig_done, 4 * u + 4)
                dve.wait_ge(v_ready, 4 * u + n + 1)
                v.tensor_tensor(gated(u, tb), av_bank[tb][:, :], gated(u, tb), ALU.mult).then_inc(w_done, 1)
                dve.wait_ge(w_done, 4 * u + n + 1)
                norm_stats(3, tb, gated(u, tb), bn4, mv4, 4 * u + n)

            def y_add_last(n):
                tb = V_ORDER[n]
                dve.wait_ge(u4_done, 4 * NT - 3 + n)
                v.tensor_tensor(x1[:, 1, tb, :], x1[:, 1, tb, :], gated(NT - 1, tb), ALU.add).then_inc(y_done, 1)

            def split(n, hi, lo):
                stage = STAGED[n]
                dve.wait_ge(s_w[n], 16)
                v.tensor_copy(hi, stage).then_inc(s_whi, 1)
                dve.wait_ge(s_whi, SPLITS.index(n) + 1)
                v.tensor_tensor(lo, stage, hi.bitcast(F32), ALU.subtract).then_inc(s_wsplit, 1)

            def first():
                v.memset(cum_carry[:, :], 0.0).then_inc(s_const, 1)
                v.memset(h_carry[:, :], 0.0).then_inc(s_const, 1)
                v.memset(x1T_carry[:, :, :], 0.0).then_inc(s_const, 1)
                v.memset(mhalf[:, :], -0.5).then_inc(s_const, 1)
                v.memset(epsilon[:, :], EPS).then_inc(s_const, 1)
                v.memset(minus1[:, :], -1.0).then_inc(s_const, 1)
                for tb in range(TB):
                    dve.wait_ge(s_x0[tb], 16)
                    ln1_block(0, 0, tb)
                dve.wait_ge(s_vec, 16)
                v.tensor_scalar(a_tmp[:, 0:1], A_v, SOFTPLUS_MAX, None, ALU.min).then_inc(s_asoft, 1)
                v.tensor_scalar(nmu, vecs[:, 3:3 + 2 * CH], -1.0, 1.0, ALU.mult, ALU.add).then_inc(s_const, 1)
                split(0, wdelta_hi[:, :, :].rearrange("p c n -> p (c n)"), wdelta_lo[:, :, :].rearrange("p c n -> p (c n)"))
                split(1, wb_hi[:, :, :].rearrange("p c n -> p (c n)"), wb_lo[:, :, :].rearrange("p c n -> p (c n)"))
                for tb in range(TB):
                    xT_lo_block(0, tb)
                split(2, wd_hi[:, :, :], wd_lo[:, :, :])
                dve.wait_ge(s_asoft, 3)
                v.tensor_scalar(a_neg[:, 0:1], a_tmp[:, 0:1], A_v, -1.0, ALU.max, ALU.mult).then_inc(s_const, 1)
                softplus_clamp(0)
                split(3, wc_hi[:, :], wc_lo[:, :])
                dve.wait_ge(s_w[4], 16)
                dve.wait_ge(s_w[5], 16)
                v.tensor_tensor(bias[:, :], STAGED[4], STAGED[5], ALU.add).then_inc(s_bias, 1)
                dve.wait_ge(s_const, CONSTANTS)
                log_decay(0, 0)
                dve.wait_ge(s_xl[1], 16)
                ln1_block(1, 1, 0)
                recurrence(0, 0)
                dve.wait_ge(s_bias, 1)
                for tb in range(1, TB):
                    ln1_block(1, 1, tb)
                ln2_stats(0, 0, 0, 0)
                ln2_stats(0, 0, 0, 1)
                dve.wait_ge(s_krv_hi, 3)
                v.tensor_tensor(wv_lo[:, :, :], STAGED[8], wv_hi[:, :, :].bitcast(F32), ALU.subtract).then_inc(s_wsplit, 1)
                xT_lo_block(1, 0)
                xT_lo_block(1, 1)
                ln2_stats(0, 0, 0, 2)
                xT_lo_block(1, 2)
                xT_lo_block(1, 3)
                ln2_stats(0, 0, 0, 3)
                ln3_stats(0, 0, 0)
                ln3_stats(0, 0, 1)
                softplus_clamp(1)
                x1n_block(0, 0, 0)
                x1n_block(0, 0, 1)
                ln3_stats(0, 0, 2)
                ln3_stats(0, 0, 3)
                x1n_block(0, 0, 2)
                x1n_block(0, 0, 3)
                for c in range(CH):
                    mix(0, 0, c)
                for c in range(CH):
                    mix_rest(0, 0, c)
                log_decay(1, 1)

            def step(t, par, j, more):
                u = t - 1
                if not isinstance(t, int) or t > 1:
                    softplus_clamp(t)
                if more:
                    ln1_stats(t + 1, 1 - par, j + par)
                if not isinstance(t, int) or t > 1:
                    log_decay(t, par)
                k_lo(u, 0)
                recurrence(t, par)
                k_lo(u, 1)
                mix(u, 1, 0)
                mix(u, 1, 1)
                k_lo(u, 2)
                mix(u, 1, 2)
                mix(u, 1, 3)
                k_lo(u, 3)
                mix_rest(u, 1, 0)
                ln2_stats(t, par, j, 0)
                if more:
                    xT_lo_block(t + 1, 0)
                mix_rest(u, 1, 1)
                ln2_stats(t, par, j, 1)
                mix_rest(u, 1, 2)
                if more:
                    xT_lo_block(t + 1, 1)
                mix_rest(u, 1, 3)
                ln2_stats(t, par, j, 2)
                if more:
                    xT_lo_block(t + 1, 2)
                ln3_stats(t, par, 0)
                ln2_stats(t, par, j, 3)
                ln3_stats(t, par, 1)
                if more:
                    xT_lo_block(t + 1, 3)
                x1n_block(t, par, 0)
                x1n_block(t, par, 1)
                ln3_stats(t, par, 2)
                ln3_stats(t, par, 3)
                x1n_block(t, par, 2)
                x1n_block(t, par, 3)
                mix(t, 0, 0)
                for c in range(CH):
                    if c < CH - 1:
                        mix(t, 0, c + 1)
                    mix_rest(t, 0, c)
                    if more:
                        gate(u, c)

            def last():
                u = NT - 1
                for c in range(CH):
                    mix(u, 1, c)
                    dve.wait_ge(mixf_done, 8 * u + 4 + c + 1)
                    v.tensor_copy(xT_hi[:, c, :], mixf[:, c, :]).then_inc(mixhi_done, 1)
                    mix_rest(u, 1, c, xT_hi, xT_lo)
                    if c:
                        k_lo(u, c - 1)
                k_lo(u, CH - 1)
                for n in range(TB):
                    gate(u - 1, n)
                dve.wait_ge(u4_done, 4 * u)
                for n in range(TB):
                    gate(u, n)
                    if n:
                        y_add_last(n - 1)
                y_add_last(TB - 1)

            run(dve, first, step, last)

        @block.gpsimd
        def _(pool):
            g = nc.gpsimd

            def scales(kind, tb, blocks, ready, n_ready, n):
                s = slice(tb, tb + blocks)
                pool.wait_ge(ready, n_ready)
                g.tensor_tensor(vare[:, kind, s], mv[:, kind, s, 1], epsilon[:, 0:blocks], ALU.add).then_inc(ve[kind], 1)
                pool.wait_ge(ve[kind], n + 1)
                g.tensor_tensor(rstd[:, kind, s], vare[:, kind, s], mhalf[:, 0:blocks], ALU.pow).then_inc(rs[kind], 1)
                if kind == 2:
                    return
                pool.wait_ge(rs[kind], n + 1)
                g.tensor_tensor(nmr[:, kind, s], mv[:, kind, s, 0], rstd[:, kind, s], ALU.mult).then_inc(nmp[kind], 1)
                pool.wait_ge(nmp[kind], n + 1)
                g.tensor_tensor(nmr[:, kind, s], nmr[:, kind, s], minus1[:, 0:blocks], ALU.mult).then_inc(nm[kind], 1)

            def ln1_pairs(t):
                for pair in range(2):
                    scales(0, 2 * pair, 2, mv1, 4 * t + 2 * pair + 2, 2 * t + pair)

            def weight_lo(n):
                pool.wait_ge(s_krv_hi, n + 1)
                g.tensor_tensor(KRV[n][1][:, :, :], STAGED[6 + n], KRV[n][0][:, :, :].bitcast(F32),
                                ALU.subtract).then_inc(s_kr_split, 1)

            def x1_scales(t, pair):
                scales(1, 2 * pair, 2, mv2, 4 * t + 2 * pair + 2, 2 * t + pair)

            def x1_add(t, par, tb):
                pool.wait_ge(u2_done, 4 * t + tb + 1)
                g.tensor_tensor(x1[:, par, tb, :], x1[:, par, tb, :], x[:, par, tb, :], ALU.add).then_inc(x1_done, 1)

            def x1n_scales(t, pair):
                scales(2, 2 * pair, 2, mv3, 4 * t + 2 * pair + 2, 2 * t + pair)

            def y_scales(u, pair):
                scales(3, V_ORDER[2 * pair], 2, mv4, 4 * u + 2 * pair + 2, 2 * u + pair)

            def y_add(u, par, n):
                tb = V_ORDER[n]
                pool.wait_ge(u4_done, 4 * u + n + 1)
                g.tensor_tensor(x1[:, par, tb, :], x1[:, par, tb, :], sig[:, tb, :], ALU.add).then_inc(y_done, 1)

            def x1_tile(t, par):
                x1_scales(t, 0)
                x1_add(t, par, 0)
                x1_add(t, par, 1)
                x1_scales(t, 1)
                x1n_scales(t, 0)
                x1_add(t, par, 2)
                x1_add(t, par, 3)
                x1n_scales(t, 1)

            def y_tile(u, par):
                for pair in range(2):
                    y_scales(u, pair)
                    y_add(u, par, 2 * pair)
                    y_add(u, par, 2 * pair + 1)

            def first():
                g.memset(ident[:, :], 0.0).then_inc(s_ident, 1)
                pool.wait_ge(s_ident, 1)
                g.affine_select(out=ident[:, :], in_=ident[:, :], compare_op=ALU.not_equal, fill=1.0, base=0,
                                pattern=[[-1, P]], channel_multiplier=1).then_inc(s_ident, 1)
                pool.wait_ge(s_const, 6)
                ln1_pairs(0)
                weight_lo(0)
                ln1_pairs(1)
                x1_tile(0, 0)
                weight_lo(1)

            def step(t, par, j, more):
                if more:
                    scales(0, 0, TB, mv1, 4 * t + 8, t + 3)
                x1_tile(t, par)
                y_tile(t - 1, 1 - par)

            def last():
                for n in range(TB):
                    scales(3, V_ORDER[n], 1, mv4, 4 * (NT - 1) + n + 1, 2 * (NT - 1) + n)

            run(pool, first, step, last)


def kernel(**inputs):
    import numpy as _np
    import concourse.bacc as _bacc
    from concourse import mybir as _mybir
    from concourse.bass_utils import run_bass_kernel_spmd as _run

    a = {n.split("_", 2)[2]: _np.asarray(v) for n, v in inputs.items()}
    n_chunks = a["mu_r"].shape[0] // 128

    def chunked(w):
        return w.reshape(w.shape[0] // 128, 128, w.shape[1]).transpose(1, 0, 2)

    def rows(b):
        return _np.broadcast_to(b[None, :], (128, b.shape[0]))

    vectors = _np.concatenate([a["A"][:, None], a["bb"][:, None], a["bdelta"][:, None],
                               a["mu_r"].reshape(n_chunks, 128).T, a["mu_k"].reshape(n_chunks, 128).T], axis=1)
    arrays = {
        "x": a["x"], "vectors": vectors, "bc": rows(a["bc"]), "bd": rows(a["bd"]),
        "w_delta": chunked(a["Wdelta"]).reshape(128, -1), "w_b": chunked(a["Wb"]).reshape(128, -1),
        "w_c": a["Wc"], "w_d": chunked(a["Wd"]),
        "w_r": chunked(a["W_r"].T), "w_k": chunked(a["W_k"].T), "w_v": chunked(a["W_v"].T),
    }
    arrays = {k: _np.ascontiguousarray(v) for k, v in arrays.items()}
    nc = _bacc.Bacc("TRN2", target_bir_lowering=False, num_devices=1, dynamic_dma_scratch_size=1024)
    args = {k: nc.dram_tensor(f"in_{k}_dram", v.shape, _mybir.dt.from_np(v.dtype), kind="ExternalInput").ap()
            for k, v in arrays.items()}
    out = nc.dram_tensor("out_dram", a["x"].shape, _mybir.dt.float32, kind="ExternalOutput").ap()
    state_space_mixer_and_channel_mixer(nc, args["x"], args["vectors"], args["bc"], args["bd"], args["w_delta"], args["w_b"],
                                        args["w_c"], args["w_d"], args["w_r"], args["w_k"], args["w_v"], out)
    r = _run(nc, [{f"in_{k}_dram": v for k, v in arrays.items()}], core_ids=[0])
    return r.results[0]["out_dram"]
```
